# Optimizing a Trainium2 kernel written in Bass

```python
import numpy as np
import jax
import jax.numpy as jnp

def _softmax(x, axis=-1):
    return jax.nn.softmax(x, axis=axis)

def _gelu(x):
    return jax.nn.gelu(x, approximate=True)

def _silu(x):
    return jax.nn.silu(x)

def _sigmoid(x):
    return jax.nn.sigmoid(x)

def _layernorm(x, axis=-1, eps=1e-05):
    m = jnp.mean(x, axis=axis, keepdims=True)
    v = jnp.var(x, axis=axis, keepdims=True)
    return (x - m) / jnp.sqrt(v + eps)

def _scatter_add(tgt, idx, src, axis=0):
    return tgt.at[idx].add(src)

def _segment_sum(src, seg, n):
    return jax.ops.segment_sum(src, seg, n)
kernel_name = 'mk_hybrid_d1_jaxref_r8_5f7747'

def setup_inputs(seed: int=0):
    np.random.seed(seed)
    _w = jnp.asarray

    def _L0_attn_a_setup():
        import jax, jax.numpy as jnp
        import numpy as np
        HEADS = 16
        PHI = (1.0 + np.sqrt(5.0)) / 2.0

        def phi_bias(L):
            pos = jnp.arange(L, dtype=jnp.float32) * PHI % 1.0
            dist = jnp.abs(pos[:, None] - pos[None, :])
            return jnp.log(jnp.exp(-dist) + 1e-08)
        key = jax.random.key(seed)
        k1, k2, k3, k4 = jax.random.split(key, 4)
        B, L, D = (2, 256, 128)
        x = jax.random.normal(k1, (B, L, D), dtype=jnp.float32)
        w_qkv = jax.random.normal(k2, (D, 3 * D), dtype=jnp.float32) * D ** (-0.5)
        w_proj = jax.random.normal(k3, (D, D), dtype=jnp.float32) * D ** (-0.5)
        b_proj = jax.random.normal(k4, (D,), dtype=jnp.float32) * 0.01
        return {'x': x, 'w_qkv': w_qkv, 'w_proj': w_proj, 'b_proj': b_proj}
    _L0_attn_a_in = _L0_attn_a_setup()

    def _L0_attn_b_setup():
        import jax, jax.numpy as jnp
        import numpy as np
        import math
        B, N, DIM, H, DH, NNULL = (2, 256, 128, 16, 64, 2)
        SCALE = 8.0
        LN_EPS = 1e-05

        def _alibi_slopes(heads):
            start = 2.0 ** (-2.0 ** (-(math.log2(heads) - 3)))
            return np.array([start * start ** i for i in range(heads)], dtype=np.float32)

        def _l2norm(t):
            n = jnp.sqrt(jnp.sum(t * t, axis=-1, keepdims=True))
            return t / jnp.maximum(n, 1e-12)
        key = jax.random.key(seed)
        ks = jax.random.split(key, 6)
        inner = H * DH
        return {'x': jax.random.normal(ks[0], (B, N, DIM), dtype=jnp.float32), 'norm_g': jnp.ones((DIM,), jnp.float32), 'norm_b': jnp.zeros((DIM,), jnp.float32), 'Wq': jax.random.normal(ks[1], (DIM, inner), jnp.float32) * 0.02, 'Wkv': jax.random.normal(ks[2], (DIM, 2 * inner), jnp.float32) * 0.02, 'q_scale': jnp.ones((DH,), jnp.float32), 'k_scale': jnp.ones((DH,), jnp.float32), 'null_kv': jax.random.normal(ks[3], (H, 2 * NNULL, DH), jnp.float32), 'Wout': jax.random.normal(ks[4], (inner, DIM), jnp.float32) * 0.02}
    _L0_attn_b_in = _L0_attn_b_setup()

    def _L0_ffn_setup():
        import jax, jax.numpy as jnp
        import numpy as np
        B, S, H, F, E = (8, 256, 128, 512, 8)
        INIT_LAMBDA = 0.2
        key = jax.random.key(seed)
        ks = jax.random.split(key, 12)
        std = 0.02
        return {'hidden_states': jax.random.normal(ks[0], (B, S, H), jnp.float32), 'gate_w1': jax.random.normal(ks[1], (H, H), jnp.float32) * 0.01, 'gate_b1': jnp.zeros((H,), jnp.float32), 'gate_w2': jax.random.normal(ks[2], (E, H), jnp.float32) * 0.01, 'gate_b2': jnp.full((E,), INIT_LAMBDA, jnp.float32), 'W1': jax.random.normal(ks[3], (F, H), jnp.float32) * std, 'b1': jax.random.normal(ks[4], (F,), jnp.float32) * std, 'W2': jax.random.normal(ks[5], (H, F), jnp.float32) * std, 'b2': jax.random.normal(ks[6], (H,), jnp.float32) * std, 'TW1': jax.random.normal(ks[7], (E, F, H), jnp.float32) * std, 'Tb1': jax.random.normal(ks[8], (E, F), jnp.float32) * std, 'TW2': jax.random.normal(ks[9], (E, H, F), jnp.float32) * std, 'Tb2': jax.random.normal(ks[10], (E, H), jnp.float32) * std}
    _L0_ffn_in = _L0_ffn_setup()
    _d = {'L0_attn_a_x': _L0_attn_a_in['x'], 'L0_attn_a_w_qkv': _L0_attn_a_in['w_qkv'], 'L0_attn_a_w_proj': _L0_attn_a_in['w_proj'], 'L0_attn_a_b_proj': _L0_attn_a_in['b_proj'], 'L0_attn_b_norm_g': _L0_attn_b_in['norm_g'], 'L0_attn_b_norm_b': _L0_attn_b_in['norm_b'], 'L0_attn_b_Wq': _L0_attn_b_in['Wq'], 'L0_attn_b_Wkv': _L0_attn_b_in['Wkv'], 'L0_attn_b_q_scale': _L0_attn_b_in['q_scale'], 'L0_attn_b_k_scale': _L0_attn_b_in['k_scale'], 'L0_attn_b_null_kv': _L0_attn_b_in['null_kv'], 'L0_attn_b_Wout': _L0_attn_b_in['Wout'], 'L0_ffn_gate_w1': _L0_ffn_in['gate_w1'], 'L0_ffn_gate_b1': _L0_ffn_in['gate_b1'], 'L0_ffn_gate_w2': _L0_ffn_in['gate_w2'], 'L0_ffn_gate_b2': _L0_ffn_in['gate_b2'], 'L0_ffn_W1': _L0_ffn_in['W1'], 'L0_ffn_b1': _L0_ffn_in['b1'], 'L0_ffn_W2': _L0_ffn_in['W2'], 'L0_ffn_b2': _L0_ffn_in['b2'], 'L0_ffn_TW1': _L0_ffn_in['TW1'], 'L0_ffn_Tb1': _L0_ffn_in['Tb1'], 'L0_ffn_TW2': _L0_ffn_in['TW2'], 'L0_ffn_Tb2': _L0_ffn_in['Tb2']}
    _x0 = _d['L0_attn_a_x']
    _d['L0_attn_a_x'] = jax.random.normal(jax.random.fold_in(jax.random.key(seed), 1), (4, 1024, 128), dtype=_x0.dtype)
    del _x0
    return _d

def reference(L0_attn_a_x, L0_attn_a_w_qkv, L0_attn_a_w_proj, L0_attn_a_b_proj, L0_attn_b_norm_g, L0_attn_b_norm_b, L0_attn_b_Wq, L0_attn_b_Wkv, L0_attn_b_q_scale, L0_attn_b_k_scale, L0_attn_b_null_kv, L0_attn_b_Wout, L0_ffn_gate_w1, L0_ffn_gate_b1, L0_ffn_gate_w2, L0_ffn_gate_b2, L0_ffn_W1, L0_ffn_b1, L0_ffn_W2, L0_ffn_b2, L0_ffn_TW1, L0_ffn_Tb1, L0_ffn_TW2, L0_ffn_Tb2):

    def _L0_attn_a_ref(x, w_qkv, w_proj, b_proj):
        import jax, jax.numpy as jnp
        import numpy as np
        HEADS = 16
        PHI = (1.0 + np.sqrt(5.0)) / 2.0

        def phi_bias(L):
            pos = jnp.arange(L, dtype=jnp.float32) * PHI % 1.0
            dist = jnp.abs(pos[:, None] - pos[None, :])
            return jnp.log(jnp.exp(-dist) + 1e-08)
        B, L, D = x.shape
        H = HEADS
        Dh = D // H
        scale = Dh ** (-0.5)
        qkv = (x @ w_qkv).reshape(B, L, 3, H, Dh)
        q = jnp.transpose(qkv[:, :, 0], (0, 2, 1, 3))
        k = jnp.transpose(qkv[:, :, 1], (0, 2, 1, 3))
        v = jnp.transpose(qkv[:, :, 2], (0, 2, 1, 3))
        attn = jnp.einsum('bhid,bhjd->bhij', q, k) * scale
        attn = attn + phi_bias(L)[None, None]
        attn = jax.nn.softmax(attn, axis=-1)
        out = jnp.einsum('bhij,bhjd->bhid', attn, v)
        out = jnp.transpose(out, (0, 2, 1, 3)).reshape(B, L, D)
        return out @ w_proj + b_proj

    def _L0_attn_b_ref(x, norm_g, norm_b, Wq, Wkv, q_scale, k_scale, null_kv, Wout):
        import jax, jax.numpy as jnp
        import numpy as np
        import math
        B, N, DIM, H, DH, NNULL = (2, 256, 128, 16, 64, 2)
        SCALE = 8.0
        LN_EPS = 1e-05

        def _alibi_slopes(heads):
            start = 2.0 ** (-2.0 ** (-(math.log2(heads) - 3)))
            return np.array([start * start ** i for i in range(heads)], dtype=np.float32)

        def _l2norm(t):
            n = jnp.sqrt(jnp.sum(t * t, axis=-1, keepdims=True))
            return t / jnp.maximum(n, 1e-12)
        b, n, dim = x.shape
        h, dh, nn = (H, DH, NNULL)
        j = n + nn
        mu = jnp.mean(x, axis=-1, keepdims=True)
        var = jnp.mean((x - mu) ** 2, axis=-1, keepdims=True)
        xn = (x - mu) * jax.lax.rsqrt(var + LN_EPS) * norm_g + norm_b
        q = (xn @ Wq).reshape(b, n, h, dh).transpose(0, 2, 1, 3)
        kv = x @ Wkv
        k, v = jnp.split(kv, 2, axis=-1)
        k = k.reshape(b, n, h, dh).transpose(0, 2, 1, 3)
        v = v.reshape(b, n, h, dh).transpose(0, 2, 1, 3)
        null = null_kv.reshape(h, nn, 2, dh)
        nk = jnp.broadcast_to(null[:, :, 0, :][None], (b, h, nn, dh))
        nv = jnp.broadcast_to(null[:, :, 1, :][None], (b, h, nn, dh))
        k = jnp.concatenate([nk, k], axis=2)
        v = jnp.concatenate([nv, v], axis=2)
        q = _l2norm(q) * q_scale
        k = _l2norm(k) * k_scale
        sim = jnp.einsum('bhid,bhjd->bhij', q, k) * SCALE
        irow = jnp.arange(j - n, j)
        jcol = jnp.arange(j)
        bias = -jnp.abs(jcol[None, :] - irow[:, None]).astype(sim.dtype)
        slopes = jnp.asarray(_alibi_slopes(h))[:, None, None]
        sim = sim + slopes * bias
        causal = jnp.triu(jnp.ones((n, j), dtype=bool), k=j - n + 1)
        neg = jnp.finfo(sim.dtype).max
        sim = jnp.where(causal[None, None], -neg, sim)
        attn = jax.nn.softmax(sim, axis=-1)
        out = jnp.einsum('bhij,bhjd->bhid', attn, v)
        out = out.transpose(0, 2, 1, 3).reshape(b, n, h * dh)
        return out @ Wout

    def _L0_ffn_ref(hidden_states, gate_w1, gate_b1, gate_w2, gate_b2, W1, b1, W2, b2, TW1, Tb1, TW2, Tb2):
        import jax, jax.numpy as jnp
        import numpy as np
        B, S, H, F, E = (8, 256, 128, 512, 8)
        INIT_LAMBDA = 0.2
        x = hidden_states
        h = jax.nn.relu(jnp.einsum('bsh,oh->bso', x, gate_w1) + gate_b1)
        g = jnp.einsum('bso,eo->bse', h, gate_w2) + gate_b2
        g = g.mean(axis=1)
        mW1 = W1 + jnp.einsum('be,efh->bfh', g, TW1)
        mb1 = b1 + g @ Tb1
        mW2 = W2 + jnp.einsum('be,ehf->bhf', g, TW2)
        mb2 = b2 + g @ Tb2
        u = jax.nn.gelu(jnp.einsum('bsh,bfh->bsf', x, mW1) + mb1[:, None, :])
        out = jnp.einsum('bsf,bhf->bsh', u, mW2) + mb2[:, None, :]
        return out
    x = L0_attn_a_x
    x = x + _L0_attn_a_ref(_layernorm(x, axis=-1), L0_attn_a_w_qkv, L0_attn_a_w_proj, L0_attn_a_b_proj)
    x = x + _L0_ffn_ref(_layernorm(x, axis=-1), L0_ffn_gate_w1, L0_ffn_gate_b1, L0_ffn_gate_w2, L0_ffn_gate_b2, L0_ffn_W1, L0_ffn_b1, L0_ffn_W2, L0_ffn_b2, L0_ffn_TW1, L0_ffn_Tb1, L0_ffn_TW2, L0_ffn_Tb2)
    x = x + _L0_attn_b_ref(_layernorm(x, axis=-1), L0_attn_b_norm_g, L0_attn_b_norm_b, L0_attn_b_Wq, L0_attn_b_Wkv, L0_attn_b_q_scale, L0_attn_b_k_scale, L0_attn_b_null_kv, L0_attn_b_Wout)
    x = x + _L0_ffn_ref(_layernorm(x, axis=-1), L0_ffn_gate_w1, L0_ffn_gate_b1, L0_ffn_gate_w2, L0_ffn_gate_b2, L0_ffn_W1, L0_ffn_b1, L0_ffn_W2, L0_ffn_b2, L0_ffn_TW1, L0_ffn_Tb1, L0_ffn_TW2, L0_ffn_Tb2)
    return x

_drawn_inputs = setup_inputs


def setup_inputs(seed=0):
    import zlib

    import numpy as np

    out = dict(_drawn_inputs(seed))
    spreads = {'L0_attn_b_norm_g': (1.0, 0.6),
     'L0_attn_b_norm_b': (0.0, 0.8),
     'L0_attn_b_q_scale': (1.0, 0.6),
     'L0_attn_b_k_scale': (1.0, 0.6),
     'L0_ffn_gate_b1': (0.0, 0.8),
     'L0_ffn_gate_b2': (0.20000000298023224, 0.6)}
    factors = {'L0_attn_a_b_proj': 5.557,
     'L0_ffn_gate_w1': 8.0,
     'L0_ffn_gate_w2': 8.0,
     'L0_ffn_b1': 5.135,
     'L0_ffn_Tb1': 8.0,
     'L0_ffn_Tb2': 2.726}
    for name, (base, spread) in spreads.items():
        noise = np.random.default_rng([zlib.crc32(name.encode()), seed]).standard_normal(out[name].shape)
        drawn = base * np.exp(spread * noise) if base else spread * noise
        out[name] = jnp.asarray(drawn.astype(out[name].dtype))
    for name, factor in factors.items():
        out[name] = (out[name] * factor).astype(out[name].dtype)
    return out
```

```python
from contextlib import ExitStack

import concourse.bass as bass
from concourse import mybir

F32 = mybir.dt.float32
F16 = mybir.dt.float16
BF16 = mybir.dt.bfloat16
ALU = mybir.AluOpType
ACT = mybir.ActivationFunctionType
AX = mybir.AxisListType
ds = bass.ds

P = 128
B, L, D = 4, 1024, 128
NT = L // P
HA, DA = 16, 8
HB, DB = 16, 64
NNULL = 2
FF, NE = 512, 8
FB = FF // P
EPS = 1e-5

A_QK = 6 * DA
A_M = A_QK
A_POS = A_M + 3
A_KPOS = A_POS + 3 * NT
A_ROWS = A_KPOS + 3 * NT
A_SPLIT_Q = [0, 0, 0, 1, 1, 2]
A_SPLIT_K = [0, 1, 2, 0, 1, 0]


def project_a(nc, t, d):
    with ExitStack() as c:
        def sb(n, s, dt): return c.enter_context(nc.sbuf_tensor("pa_" + n, s, dt))
        def ps(n, s, dt): return c.enter_context(nc.psum_tensor("pa_" + n, s, dt))

        x = sb("x", [P, B, NT, D], F32)
        wqkv = sb("w", [P, 3 * D], F32)
        stats, mv = sb("stats", [P, NT, 6], F32), sb("mv", [P, NT, 2], F32)
        var, std, rstd = (sb(n, [P, NT], F32) for n in ("var", "std", "rstd"))
        xn = sb("xn", [P, NT, D], F32)
        xnT = sb("xnT", [P, L], F32)
        rest = sb("rest", [P, 2, 2, L], F32)
        parts = sb("parts", [P, 2, 2, 3, L], BF16)
        psT = ps("psT", [P, L], F32)
        psQK = [ps(f"ps{n}", [P, L], F32) for n in "qk"]
        psV = ps("psV", [P, L], F32)
        s = {n: c.enter_context(nc.semaphore("pa_" + n)) for n in (
            "x_loaded w_loaded scaled ones var_ready std_ready xn_ready xn_turned xnT_copied qk_ready v_ready "
            "part1 rest_ready part2 part3 v_copied step stored0 stored1").split()}
        block = c.enter_context(nc.Block())

        @block.sync
        def _(sp):
            for b in range(B):
                sp.dma_start(x[:, b], d["x_sorted"][b].rearrange("(t p) e -> p t e", p=P)).then_inc(s["x_loaded"], 16)
                if b == 0:
                    sp.wait_ge(s["x_loaded"], 16)
                    sp.dma_start(t["identf"][:], d["identf"]).then_inc(s["w_loaded"], 16)
                    sp.dma_start(wqkv[:], d["w_qkv"]).then_inc(s["w_loaded"], 16)
            for b in range(B):
                for i in range(2):
                    sp.wait_ge(s["part3"], 2 * b + i + 1)
                    sp.dma_start(d["parts"][b * 2 + i].rearrange("s p q -> p s q"), parts[:, b % 2, i])\
                      .then_inc(s[f"stored{b % 2}"], 16)
            for i in range(2):
                sp.wait_ge(s[f"stored{i}"], 16 * B)

        @block.vector
        def _(dve):
            v = nc.vector
            st = Steps(s["step"], 0)

            def run(ins):
                dve.wait_ge(s["step"], st.after(ins))

            def normalize(b):
                if b < 2:
                    dve.wait_ge(s["x_loaded"], 16 if b == 0 else 16 * B)
                for i in range(NT):
                    ins = v.bn_stats(stats[:, i, :], x[:, b, i, :])
                run(ins)
                for i in range(NT):
                    ins = v.bn_aggr(mv[:, i, :], stats[:, i, :])
                run(ins)
                v.tensor_scalar(var[:], mv[:, :, 1], EPS, None, ALU.add).then_inc(s["var_ready"], 1)
                dve.wait_ge(s["std_ready"], b + 1)
                run(v.reciprocal(rstd[:], std[:]))
                if b:
                    dve.wait_ge(s["xn_turned"], b)
                for i in range(NT):
                    ins = v.tensor_scalar(xn[:, i, :], x[:, b, i, :], mv[:, i, 0:1], rstd[:, i:i + 1],
                                          ALU.subtract, ALU.mult)
                ins.then_inc(s["xn_ready"], 1)
                dve.wait_ge(s["xn_ready"], b + 1)

            normalize(0)
            dve.wait_ge(s["w_loaded"], 32)
            v.tensor_scalar(wqkv[:, 0:D], wqkv[:, 0:D], float(DA) ** -0.5, None, ALU.mult).then_inc(s["scaled"], 1)
            for b in range(B):
                if b + 1 < B:
                    normalize(b + 1)
                for i in range(2):
                    dve.wait_ge(s["part1"], 2 * b + i + 1)
                    if b >= 2:
                        dve.wait_ge(s["part3"], 2 * b + i - 3)
                    v.tensor_tensor(rest[:, b % 2, i], psQK[i][:], parts[:, b % 2, i, 0], ALU.subtract)\
                     .then_inc(s["rest_ready"], 1)

        @block.gpsimd
        def _(pool):
            nc.gpsimd.memset(t["v_a"][:, :, :, DA:DA + 1], 1.0)
            for b in range(B):
                for i in range(2):
                    pool.wait_ge(s["part2"], 2 * b + i + 1)
                    nc.gpsimd.tensor_tensor(parts[:, b % 2, i, 2], rest[:, b % 2, i], parts[:, b % 2, i, 1],
                                            ALU.subtract).then_inc(s["part3"], 1)

        @block.scalar
        def _(act):
            a = nc.scalar

            def root(b):
                act.wait_ge(s["var_ready"], b + 1)
                a.activation(std[:], var[:], ACT.Sqrt).then_inc(s["std_ready"], 1)

            def copy_xn(b):
                act.wait_ge(s["xn_turned"], b + 1)
                if b:
                    act.wait_ge(s["v_ready"], b)
                a.activation(xnT[:], psT[:], ACT.Copy).then_inc(s["xnT_copied"], 1)

            root(0)
            copy_xn(0)
            for b in range(B):
                if b + 1 < B:
                    root(b + 1)
                for i in range(2):
                    act.wait_ge(s["qk_ready"], 2 * b + i + 1)
                    if b >= 2 and i == 0:
                        act.wait_ge(s[f"stored{b % 2}"], 32 * (b // 2))
                    a.activation(parts[:, b % 2, i, 0], psQK[i][:], ACT.Copy).then_inc(s["part1"], 1)
                act.wait_ge(s["v_ready"], b + 1)
                a.activation(t["v_a"][:, :, b * HA:(b + 1) * HA, 0:DA],
                             psV[:].rearrange("p (t h e) -> p t h e", t=NT, e=DA), ACT.Copy).then_inc(s["v_copied"], 1)
                if b + 1 < B:
                    copy_xn(b + 1)
                for i in range(2):
                    act.wait_ge(s["rest_ready"], 2 * b + i + 1)
                    a.activation(parts[:, b % 2, i, 1], rest[:, b % 2, i], ACT.Copy).then_inc(s["part2"], 1)

        @block.tensor
        def _(pe):
            m = nc.tensor

            def turn_xn(b):
                pe.wait_ge(s["xn_ready"], b + 1)
                if b:
                    pe.wait_ge(s["xnT_copied"], b)
                for i in range(NT):
                    ins = m.transpose(psT[:, i * P:(i + 1) * P], xn[:, i, :], t["identf"][:])
                ins.then_inc(s["xn_turned"], 1)

            pe.wait_ge(s["w_loaded"], 32)
            turn_xn(0)
            pe.wait_ge(s["scaled"], 1)
            for b in range(B):
                pe.wait_ge(s["xnT_copied"], b + 1)
                for i in range(2):
                    if b:
                        pe.wait_ge(s["rest_ready"], 2 * b + i - 1)
                    for j in range(2):
                        ins = m.matmul(psQK[i][:, j * 512:j * 512 + 512], wqkv[:, i * D:i * D + D],
                                       xnT[:, j * 512:j * 512 + 512], start=True, stop=True)
                    ins.then_inc(s["qk_ready"], 1)
                if b:
                    pe.wait_ge(s["v_copied"], b)
                for i in range(NT):
                    ins = m.matmul(psV[:, i * P:(i + 1) * P], xnT[:, i * P:(i + 1) * P], wqkv[:, 2 * D:3 * D],
                                   start=True, stop=True)
                ins.then_inc(s["v_ready"], 1)
                if b + 1 < B:
                    turn_xn(b + 1)


class Steps:

    def __init__(self, sem, base):
        self.sem, self.base, self.n = sem, base, 0

    def after(self, ins):
        ins.then_inc(self.sem, 1)
        self.n += 1
        return self.base + self.n


FFN_LOADS = {"gate": ("gw1", "gb1", "gw2", "gb2row", "gb2col", "tb2", "b2", "ones"),
             "up": ("w1", "tb1", "b1", "tw1"), "down": ("w2", "tw2")}


def ffn_tiles(nc, c, name, project):
    def sb(n, s, dt): return c.enter_context(nc.sbuf_tensor(f"{name}_{n}", s, dt))
    t = {"tw1": sb("tw1", [P, NE, FF], F32), "tw2": sb("tw2", [P, NE, FF], F32),
         "w1": sb("w1", [P, FF], F32), "w2": sb("w2", [P, FF], F32), "gw1": sb("gw1", [P, D], F32),
         "gb1": sb("gb1", [P, 1], F32), "gw2": sb("gw2", [P, NE], F32), "gb2row": sb("gb2row", [P, NE], F32),
         "gb2col": sb("gb2col", [NE, 1], F32), "b1": sb("b1", [P, FB], F32), "tb1": sb("tb1", [P, FB, NE], F32),
         "tb2": sb("tb2", [NE, D], F32), "b2": sb("b2", [1, D], F32), "ones": sb("ones", [1, P], F32)}
    if project:
        t.update({"wproj": sb("wproj", [P, D], F32), "bproj": sb("bproj", [P, D], F32),
                  "perm": sb("perm", [P, NT, L], BF16)})
    return t


def layer_norm(v, dve, steps, wait_sem, x, xn, w, std_sem, std_count, var_sem):
    dve.sem_inc(w["pad"], 1)
    for i in range(NT):
        s = v.bn_stats(w["stats"][:, i, :], x(i))
    dve.wait_ge(wait_sem, steps.after(s))
    dve.sem_inc(w["pad"], 1)
    for i in range(NT):
        s = v.bn_aggr(w["mv"][:, i, :], w["stats"][:, i, :])
    dve.wait_ge(wait_sem, steps.after(s))
    v.tensor_scalar(w["var"][:], w["mv"][:, :, 1], EPS, None, ALU.add).then_inc(var_sem, 1)
    dve.wait_ge(std_sem, std_count)
    dve.wait_ge(wait_sem, steps.after(v.reciprocal(w["rstd"][:], w["std"][:])))
    for i in range(NT):
        s = v.tensor_scalar(xn[:, i, :], x(i), w["mv"][:, i, 0:1], w["rstd"][:, i:i + 1], ALU.subtract, ALU.mult)
    return s


def norm_buffers(sb, name, pad):
    return {"stats": sb(name + "_stats", [P, NT, 6], F32), "mv": sb(name + "_mv", [P, NT, 2], F32),
            "var": sb(name + "_var", [P, NT], F32), "std": sb(name + "_std", [P, NT], F32),
            "rstd": sb(name + "_rstd", [P, NT], F32), "pad": pad}


def ffn(nc, t, d, to, also, name, project):
    with ExitStack() as c:
        def sb(n, s, dt): return c.enter_context(nc.sbuf_tensor(f"{name}_{n}", s, dt))
        def ps(n, s, dt): return c.enter_context(nc.psum_tensor(f"{name}_{n}", s, dt))

        opart = sb("opart", [P, 3, NT, P], BF16) if project else None
        orest = sb("orest", [P, NT, P], F32) if project else None
        oT = sb("oT", [P, L], F32) if project else None
        stats, mv = sb("stats", [P, NT, 6], F32), sb("mv", [P, NT, 2], F32)
        var, std, rstd = (sb(n, [P, NT], F32) for n in ("var", "std", "rstd"))
        xn = sb("xn", [P, NT, D], F32)
        xnT = [sb(f"xnT{i}", [P, L], F32) for i in range(2)]
        hrelu = sb("hrelu", [P, 512], F32)
        hsum = sb("hsum", [P, 2], F32)
        hmean = sb("hmean", [P, 1], F32)
        hwide = sb("hwide", [P, P], F32)
        g = sb("g", [P, NE], F32)
        gcol = sb("gcol", [NE, P], F32)
        mw1 = [sb(f"mw1{i}", [P, FF], F32) for i in range(2)]
        mw2 = [sb(f"mw2{i}", [P, FF], F32) for i in range(2)]
        gb = sb("gb", [P, FB, NE], F32)
        mb1 = [sb(f"mb1{i}", [P, FB], F32) for i in range(2)]
        mb2 = [sb(f"mb2{i}", [P, D], F32) for i in range(2)]
        u = sb("u", [P, 2, FB, 512], F32)
        psT = ps("psT", [P, L], F32)
        psG = ps("psG", [P, L], F32)
        psU = [ps(f"psU{i}", [P, 512], F32) for i in range(2)]
        psD = [ps(f"psD{i}", [P, 512], F32) for i in range(2)]
        s = {n: c.enter_context(nc.semaphore(f"{name}_{n}")) for n in (
            "opart oT_turned oT_copied projected x_in var_ready std_ready xn_ready xn_turned xnT_copied gated relu "
            "hwide g_summed gcol_summed g_ready gcol_ready mb2_summed mw1_ready mb1_ready mw2_ready mb2_ready "
            "up gelu down x_done step stored also_loaded proj_loaded x_loaded gate_loaded up_loaded down_loaded").split()}

        def loaded(engine, what):
            count = {"proj": 2, "x": 1 + B}.get(what) or len(FFN_LOADS[what])
            if project or what not in ("proj", "x"):
                engine.wait_ge(s[what + "_loaded"], 16 * count)

        with nc.Block() as block:
            @block.vector
            def _(dve):
                v = nc.vector
                st = Steps(s["step"], 0)

                def run(ins):
                    dve.wait_ge(s["step"], st.after(ins))

                def x_of(b):
                    return t["x"][:, b, :, :]

                def split_out(b):
                    o = t["o_a"][:, :, b * HA:(b + 1) * HA, :].rearrange("p t h e -> p t (h e)")
                    if b:
                        dve.wait_ge(s["oT_turned"], b)
                    run(v.tensor_copy(opart[:, 0, :, :], o))
                    run(v.tensor_tensor(orest[:], o, opart[:, 0, :, :], ALU.subtract))
                    run(v.tensor_copy(opart[:, 1, :, :], orest[:]))
                    v.tensor_tensor(opart[:, 2, :, :], orest[:], opart[:, 1, :, :], ALU.subtract).then_inc(s["opart"], 1)
                    loaded(dve, "x")
                    run(v.tensor_tensor(x_of(b), x_of(b), t["bproj"][:].unsqueeze(1).broadcast_to([P, NT, D]), ALU.add))

                def normalize(b):
                    if project:
                        dve.wait_ge(s["projected"], b + 1)
                        v.tensor_tensor(x_of(b), x_of(b), psG[:].rearrange("p (t e) -> p t e", e=D), ALU.add)\
                         .then_inc(s["x_in"], 1)
                        dve.wait_ge(s["x_in"], b + 1)
                    for i in range(NT):
                        ins = v.bn_stats(stats[:, i, :], t["x"][:, b, i, :])
                    run(ins)
                    for i in range(NT):
                        ins = v.bn_aggr(mv[:, i, :], stats[:, i, :])
                    run(ins)
                    v.tensor_scalar(var[:], mv[:, :, 1], EPS, None, ALU.add).then_inc(s["var_ready"], 1)
                    dve.wait_ge(s["std_ready"], b + 1)
                    run(v.reciprocal(rstd[:], std[:]))
                    if b:
                        dve.wait_ge(s["xn_turned"], b)
                    for i in range(NT):
                        ins = v.tensor_scalar(xn[:, i, :], t["x"][:, b, i, :], mv[:, i, 0:1], rstd[:, i:i + 1],
                                              ALU.subtract, ALU.mult)
                    ins.then_inc(s["xn_ready"], 1)
                    dve.wait_ge(s["xn_ready"], b + 1)

                def gate(b):
                    dve.wait_ge(s["relu"], 2 * b + 2)
                    run(v.tensor_tensor(hmean[:], hsum[:, 0:1], hsum[:, 1:2], ALU.add))
                    v.tensor_scalar(hwide[:], hmean[:].broadcast_to([P, P]), 1.0 / L, None, ALU.mult)\
                     .then_inc(s["hwide"], 1)
                    dve.wait_ge(s["g_summed"], b + 1)
                    v.tensor_tensor(g[:], psG[:, 0:NE], t["gb2row"][:], ALU.add).then_inc(s["g_ready"], 1)
                    dve.wait_ge(s["g_ready"], b + 1)

                def mix(dst, src, base, ready):
                    for e in range(NE):
                        ins = v.scalar_tensor_tensor(out=dst[:], in0=src[:, e, :], scalar=g[:, e:e + 1],
                                                     in1=(base if e == 0 else dst)[:], op0=ALU.mult, op1=ALU.add)
                        if e < NE - 1:
                            run(ins)
                    ins.then_inc(ready, 1)

                def weights_up(b):
                    if b >= 2:
                        dve.wait_ge(s["down"], 2 * b - 2)
                    mix(mw1[b % 2], t["tw1"], t["w1"], s["mw1_ready"])
                    dve.wait_ge(s["mb2_summed"], b + 1)
                    v.tensor_copy(mb2[b % 2][:], psG[:, 0:D]).then_inc(s["mb2_ready"], 1)
                    run(v.tensor_tensor(gb[:], t["tb1"][:], g[:].unsqueeze(1).broadcast_to([P, FB, NE]), ALU.mult))
                    run(v.tensor_reduce(mb1[b % 2][:], gb[:], AX.X, ALU.add))
                    v.tensor_tensor(mb1[b % 2][:], mb1[b % 2][:], t["b1"][:], ALU.add).then_inc(s["mb1_ready"], 1)

                def weights_down(b):
                    mix(mw2[b % 2], t["tw2"], t["w2"], s["mw2_ready"])
                    dve.wait_ge(s["mb2_ready"], b + 1)
                    run(v.tensor_tensor(x_of(b), x_of(b), mb2[b % 2][:].unsqueeze(1).broadcast_to([P, NT, D]), ALU.add))

                def add_down(b, j):
                    xh = t["x"][:, b, j * 4:j * 4 + 4, :]
                    dve.wait_ge(s["down"], 2 * b + j + 1)
                    v.tensor_tensor(xh, xh, psD[j][:].rearrange("p (t e) -> p t e", e=D), ALU.add).then_inc(s["x_done"], 1)

                def ready(b):
                    gate(b)
                    if project and b + 1 < B:
                        split_out(b + 1)
                    if b == 0:
                        loaded(dve, "up")
                    weights_up(b)
                    if b == 0:
                        loaded(dve, "down")
                    if project:
                        weights_down(b)
                    if b + 1 < B:
                        normalize(b + 1)
                    if not project:
                        weights_down(b)

                if project:
                    split_out(0)
                normalize(0)
                loaded(dve, "gate")
                ready(0)
                for b in range(B):
                    if b + 1 < B:
                        ready(b + 1)
                    add_down(b, 0)
                    add_down(b, 1)

            @block.scalar
            def _(act):
                a = nc.scalar

                def copy_out(b):
                    act.wait_ge(s["oT_turned"], b + 1)
                    if b:
                        act.wait_ge(s["projected"], b)
                    a.activation(oT[:], psT[:], ACT.Copy).then_inc(s["oT_copied"], 1)

                def root(b):
                    act.wait_ge(s["var_ready"], b + 1)
                    a.activation(std[:], var[:], ACT.Sqrt).then_inc(s["std_ready"], 1)

                def copy_xn(b):
                    act.wait_ge(s["xn_turned"], b + 1)
                    if b >= 2:
                        act.wait_ge(s["up"], 8 * b - 8)
                    a.activation(xnT[b % 2][:], psT[:], ACT.Copy).then_inc(s["xnT_copied"], 1)

                def gate(b):
                    for j in range(2):
                        act.wait_ge(s["gated"], 2 * b + j + 1)
                        if b or j:
                            act.wait_ge(s["relu"], 2 * b + j)
                        if b and j == 0:
                            act.wait_ge(s["hwide"], b)
                        a.activation(hrelu[:], psG[:, j * 512:j * 512 + 512], ACT.Relu, bias=t["gb1"][:, 0:1],
                                     accum_out=hsum[:, j:j + 1]).then_inc(s["relu"], 1)

                def gates(b):
                    act.wait_ge(s["gcol_summed"], b + 1)
                    a.activation(gcol[:], psG[0:NE, 512:512 + P], ACT.Identity, bias=t["gb2col"][:, 0:1])\
                     .then_inc(s["gcol_ready"], 1)

                def gelu(b, j):
                    if j == 0:
                        act.wait_ge(s["mb1_ready"], b + 1)
                    if b:
                        act.wait_ge(s["down"], 2 * b - 1 + j)
                    for f in range(FB):
                        act.wait_ge(s["up"], 8 * b + 4 * j + f + 1)
                        a.activation(u[:, j, f, :], psU[f % 2][:], ACT.Gelu_apprx_tanh, bias=mb1[b % 2][:, f:f + 1])\
                         .then_inc(s["gelu"], 1)

                def prepare(b):
                    if b < B:
                        if project:
                            copy_out(b)
                        root(b)

                prepare(0)
                copy_xn(0)
                loaded(act, "gate")
                gate(0)
                gates(0)
                prepare(1)
                for b in range(B):
                    gelu(b, 0)
                    if b + 1 < B:
                        copy_xn(b + 1)
                        gate(b + 1)
                    gelu(b, 1)
                    if b + 1 < B:
                        gates(b + 1)
                    prepare(b + 2)

            @block.tensor
            def _(pe):
                m = nc.tensor

                def turn_out(b):
                    pe.wait_ge(s["opart"], b + 1)
                    if b:
                        pe.wait_ge(s["xnT_copied"], b)
                    for j in range(2):
                        for i in range(NT):
                            for k in range(3):
                                ins = m.matmul(psT[:, j * 512:j * 512 + 512], opart[:, k, i, :],
                                               t["perm"][:, i, j * 512:j * 512 + 512],
                                               start=(i == k == 0), stop=(i == NT - 1 and k == 2))
                    ins.then_inc(s["oT_turned"], 1)

                def project_out(b):
                    pe.wait_ge(s["oT_copied"], b + 1)
                    if b:
                        pe.wait_ge(s["mb2_ready"], b)
                    for i in range(NT):
                        ins = m.matmul(psG[:, i * P:(i + 1) * P], oT[:, i * P:(i + 1) * P], t["wproj"][:],
                                       start=True, stop=True)
                    ins.then_inc(s["projected"], 1)

                def turn_xn(b):
                    pe.wait_ge(s["xn_ready"], b + 1)
                    if project:
                        pe.wait_ge(s["oT_copied"], b + 1)
                    elif b:
                        pe.wait_ge(s["xnT_copied"], b)
                    for i in range(NT):
                        ins = m.transpose(psT[:, i * P:(i + 1) * P], xn[:, i, :], t["identf"][:])
                    ins.then_inc(s["xn_turned"], 1)

                def gate(b):
                    pe.wait_ge(s["xnT_copied"], b + 1)
                    if project:
                        pe.wait_ge(s["x_in"], b + 1)
                    if b:
                        pe.wait_ge(s["mb2_ready"], b)
                        pe.wait_ge(s["gcol_ready"], b)
                    for j in range(2):
                        m.matmul(psG[:, j * 512:j * 512 + 512], t["gw1"][:], xnT[b % 2][:, j * 512:j * 512 + 512],
                                 start=True, stop=True).then_inc(s["gated"], 1)

                def gates(b):
                    pe.wait_ge(s["relu"], 2 * b + 2)
                    pe.wait_ge(s["hwide"], b + 1)
                    m.matmul(psG[:, 0:NE], hwide[:], t["gw2"][:], start=True, stop=True).then_inc(s["g_summed"], 1)
                    m.matmul(psG[0:NE, 512:512 + P], t["gw2"][:], hwide[:], start=True, stop=True)\
                     .then_inc(s["gcol_summed"], 1)
                    pe.wait_ge(s["gcol_ready"], b + 1)
                    pe.wait_ge(s["g_ready"], b + 1)
                    m.matmul(psG[:, 0:D], gcol[:], t["tb2"][:], start=True, stop=False)
                    m.matmul(psG[:, 0:D], t["ones"][0:1, :], t["b2"][:], start=False, stop=True)\
                     .then_inc(s["mb2_summed"], 1)

                def up(b, j):
                    if j == 0:
                        pe.wait_ge(s["mw1_ready"], b + 1)
                    for f in range(FB):
                        n = 8 * b + 4 * j + f
                        if n >= 2:
                            pe.wait_ge(s["gelu"], n - 1)
                        m.matmul(psU[f % 2][:], mw1[b % 2][:, f * P:(f + 1) * P], xnT[b % 2][:, j * 512:j * 512 + 512],
                                 start=True, stop=True).then_inc(s["up"], 1)

                def down(b, j):
                    pe.wait_ge(s["gelu"], 8 * b + 4 * j + 4)
                    if j == 0:
                        pe.wait_ge(s["mw2_ready"], b + 1)
                    if b:
                        pe.wait_ge(s["x_done"], 2 * b - 1 + j)
                    for i in range(4):
                        for f in range(FB):
                            ins = m.matmul(psD[j][:, i * P:(i + 1) * P], u[:, j, f, i * P:(i + 1) * P],
                                           mw2[b % 2][:, f * P:(f + 1) * P], start=(f == 0), stop=(f == FB - 1))
                    ins.then_inc(s["down"], 1)

                def prepare(b):
                    if project and b < B:
                        turn_out(b)
                        project_out(b)

                loaded(pe, "proj")
                prepare(0)
                turn_xn(0)
                loaded(pe, "gate")
                gate(0)
                gates(0)
                prepare(1)
                for b in range(B):
                    up(b, 0)
                    if b + 1 < B:
                        turn_xn(b + 1)
                        gate(b + 1)
                    up(b, 1)
                    if b + 1 < B:
                        gates(b + 1)
                    if project and b + 2 < B:
                        turn_out(b + 2)
                    down(b, 0)
                    if project and b + 2 < B:
                        project_out(b + 2)
                    down(b, 1)

            @block.sync
            def _(sp):
                if project:
                    for n in ("perm", "wproj"):
                        sp.dma_start(t[n][:], d[n]).then_inc(s["proj_loaded"], 16)
                    sp.dma_start(t["bproj"][:], d["bproj"].broadcast_to([P, D])).then_inc(s["x_loaded"], 16)
                    for b in range(B):
                        sp.dma_start(t["x"][:, b], d["x"][b].rearrange("(t p) e -> p t e", p=P)).then_inc(s["x_loaded"], 16)
                for what, names in FFN_LOADS.items():
                    for n in names:
                        of = d[n].broadcast_to([P, NE]) if n == "gb2row" else d[n]
                        sp.dma_start(t[n][:], of).then_inc(s[what + "_loaded"], 16)
                for n in also:
                    sp.dma_start(t[n][:], d[n]).then_inc(s["also_loaded"], 16)
                if also:
                    sp.wait_ge(s["also_loaded"], 16 * len(also))
                if to is not None:
                    for b in range(B):
                        sp.wait_ge(s["x_done"], 2 * b + 2)
                        sp.dma_start(to[b].rearrange("(t p) e -> p t e", p=P), t["x"][:, b]).then_inc(s["stored"], 16)
                    sp.wait_ge(s["stored"], 16 * B)


def attend_a(nc, t, d, g):
    NPAIR = HA
    FIRST = 4
    NLOAD = 12 * 16
    NCONST = 4
    AHEAD = 6
    LAST = NT - 1 - AHEAD // 2
    TURN = LAST + 2
    VW = 32

    def events(i):
        out = []
        for kb in range(NT):
            ahead = 1 if kb <= LAST else 2
            if i + ahead < NPAIR:
                out += [(kb, "max", j) for j in range(2)]
            if kb == 3 and i > 0:
                out.append((kb, "out", 0))
            if kb == TURN and i + 1 < NPAIR:
                out.append((kb, "turn", 0))
        return out

    first = 2 * NT + 1 + AHEAD
    start = {0: first}
    for n in range(NPAIR):
        start[n + 1] = start[n] + len(events(n))

    def use(i, kb, kind, tile=0):
        r = start[i] + events(i).index((kb, kind, tile))
        return r, r % 2

    def use_of_turn(p):
        return (2 * NT, 0) if p == 0 else use(p - 1, TURN, "turn")

    with ExitStack() as c:
        def sb(n, s, dt): return c.enter_context(nc.sbuf_tensor(n, s, dt))
        def ps(n, s, dt): return c.enter_context(nc.psum_tensor(n, s, dt))
        def sem(n): return c.enter_context(nc.semaphore(n))

        q = sb("aa_q", [A_ROWS, 2 * HA, L], BF16)
        k = sb("aa_k", [A_ROWS, 2 * HA, L], BF16)
        near = sb("aa_near", [P, NT, P], F32)
        prob = sb("aa_prob", [P, 4, 2, L], F32)
        vst = sb("aa_vst", [P, 2, NT, 2, VW], F32)
        mx = sb("aa_mx", [P, 2 * NT], F32)
        mrest = sb("aa_mrest", [P, 2 * NT], F32)
        mparts = sb("aa_mparts", [P, P // (2 * NT), 2 * NT], BF16)
        mT = sb("aa_mT", [3 * 2 * NT, P], BF16)
        oT = sb("aa_oT", [P, 512], F32)
        rsum = sb("aa_rsum", [P, NT // 2, 4], F32)
        warm = sb("aa_warm", [P, 1], F32)
        psS = [ps(f"aa_psS{i}", [P, 512], F32) for i in range(3)]
        psM = [ps(f"aa_psM{i}", [P, L], F32) for i in range(2)]
        psO = ps("aa_psO", [P, 512], F32)
        (consts, loaded, s_ready, exp_done, near_done, pv_done, use_ready, use_done, m_split, m_loaded,
         v_zeroed, m_zeroed, v_staged, oT_ready, inverted) = (t["sems_a"][n] for n in A_SEMS)
        block = c.enter_context(nc.Block())

        @block.sync
        def _(sp):
            def load(b, first, last):
                for i in range(6):
                    for side, to, of in ((0, q, A_SPLIT_Q[i]), (1, k, A_SPLIT_K[i])):
                        src = d["parts"][ds(g * 4 + b * 2 + side, 1), of, first * DA:last * DA, :]
                        sp.dma_start(to[i * DA:(i + 1) * DA, b * HA + first:b * HA + last, :],
                                     src.rearrange("o (h e) q -> e (o h) q", e=DA)).then_inc(loaded, 16)

            load(0, 0, FIRST)
            sp.wait_ge(loaded, NLOAD)
            sp.dma_start(k[A_M:A_ROWS], d["a_krows"].unsqueeze(1).broadcast_to([A_ROWS - A_M, 2 * HA, L]))\
              .then_inc(consts, 16)
            sp.dma_start(q[A_POS:A_ROWS], d["a_qrows"].unsqueeze(1).broadcast_to([A_ROWS - A_POS, 2 * HA, L]))\
              .then_inc(consts, 16)
            sp.dma_start(near[:], d["near"]).then_inc(consts, 16)
            sp.dma_start(t["identb"][:], d["identb"]).then_inc(consts, 16)
            load(0, FIRST, HA)
            for p in range(NPAIR):
                if p == 1:
                    sp.wait_ge(loaded, 2 * NLOAD)
                    load(1, 0, HA)
                sp.wait_ge(use_done, use_of_turn(p)[0] + 1)
                for s in range(3):
                    to = q[A_M + s:A_M + s + 1, p * 2:p * 2 + 2, :].rearrange("r h (i e) -> r (h i) e", e=P)
                    sp.dma_start(to, mT[s * 2 * NT:(s + 1) * 2 * NT, :]).then_inc(m_loaded, 16)
                sp.wait_ge(m_loaded, 48 * p + 48)
            sp.wait_ge(loaded, 3 * NLOAD)

        @block.gpsimd
        def _(pool):
            nc.gpsimd.memset(vst[:], 0.0).then_inc(v_zeroed, 1)
            pool.wait_ge(v_zeroed, 1)

            def stage(i, odd):
                if i >= 2:
                    pool.wait_ge(pv_done, i * NT - NT)
                nc.gpsimd.tensor_copy(vst[:, odd, :, :, 0:DA + 1], t["v_a"][:, :, ds(g * 2 * HA + i * 2, 2), :])\
                  .then_inc(v_staged, 1)

            def pair(i, odd):
                for kb in range(NT):
                    pool.wait_ge(exp_done, (i * NT + kb) * 4 + 3 + kb // (NT // 2))
                    p = prob[:, kb % 4, :, kb * P:(kb + 1) * P]
                    nc.gpsimd.tensor_tensor(p, p, near[:, kb, :].unsqueeze(1).broadcast_to([P, 2, P]), ALU.mult)\
                      .then_inc(near_done, 1)
                    if kb == 3 and i < NPAIR - 1:
                        stage(i + 1, 1 - odd)

            stage(0, 0)
            pool.wait_ge(consts, 16 * NCONST)
            for i in range(NPAIR):
                pair(i, i % 2)

        @block.scalar
        def _(act):
            nc.scalar.activation(warm[:], t["identf"][:, 0:1], ACT.Exp)

            def take_out(i, odd):
                act.wait_ge(pv_done, i * NT + NT)
                if i > 0:
                    act.wait_ge(use_ready, use(i, 3, "out")[0] + 1)
                nc.scalar.activation(oT[:], psO[:], ACT.Copy).then_inc(oT_ready, 1)

            def pair(i, odd):
                for kb in range(NT):
                    at = i * NT + kb
                    for h in range(2):
                        for half in range(2):
                            act.wait_ge(s_ready, at * 4 + 2 * h + half + 1)
                            if h == half == 0 and at >= 4:
                                act.wait_ge(pv_done, at - 3)
                            nc.scalar.activation(prob[:, kb % 4, h, half * 512:half * 512 + 512],
                                                 psS[(at * 4 + 2 * h + half) % 3][:],
                                                 ACT.Exp).then_inc(exp_done, 1)
                    if kb == 1 and i > 0:
                        take_out(i - 1, 1 - odd)

            for i in range(NPAIR):
                pair(i, i % 2)
            take_out(NPAIR - 1, 1)

        @block.vector
        def _(dve):
            v = nc.vector

            def maximum(p, tile, r, which):
                dve.wait_ge(use_ready, r + 1)
                if tile == 0 and p > 0:
                    dve.wait_ge(m_split, 4 * p)
                v.tensor_reduce(mx[:, tile:tile + 1], psM[which][:], AX.X, ALU.max,
                                negate=True).then_inc(use_done, 1)

            def split(p, r):
                dve.wait_ge(use_done, r + 1)
                v.tensor_copy(mparts[:, 0, :], mx[:]).then_inc(m_split, 1)
                dve.wait_ge(m_split, 4 * p + 1)
                v.tensor_tensor(mrest[:], mx[:], mparts[:, 0, :], ALU.subtract).then_inc(m_split, 1)
                dve.wait_ge(m_split, 4 * p + 2)
                v.tensor_copy(mparts[:, 1, :], mrest[:]).then_inc(m_split, 1)
                dve.wait_ge(m_split, 4 * p + 3)
                v.tensor_tensor(mparts[:, 2, :], mrest[:], mparts[:, 1, :], ALU.subtract).then_inc(m_split, 1)

            def take_turned(p):
                r, which = use_of_turn(p)
                dve.wait_ge(use_ready, r + 1)
                if p > 0:
                    dve.wait_ge(m_loaded, 48 * p)
                v.tensor_copy(mT[:], psM[which][0:3 * 2 * NT, 0:P // 2].bitcast(BF16)).then_inc(use_done, 1)

            def normalize(i, r, which):
                o = psM[which][:, 0:4 * P].rearrange("p (c g e) -> p c g e", c=NT // 2, e=VW)
                dve.wait_ge(use_ready, r + 1)
                v.reciprocal(rsum[:], o[:, :, :, DA]).then_inc(inverted, 1)
                dve.wait_ge(inverted, 2 * i + 1)
                for h in range(2):
                    to = t["o_a"][:, :, ds(g * 2 * HA + i * 2 + h, 1), :].rearrange("p (f c) o e -> p f c (o e)", f=2)
                    s = v.tensor_tensor(to, o[:, :, 2 * h:2 * h + 2, 0:DA].rearrange("p c f e -> p f c e"),
                                        rsum[:, :, 2 * h:2 * h + 2].rearrange("p c f -> p f c").unsqueeze(3)
                                        .broadcast_to([P, 2, NT // 2, DA]), ALU.mult)
                    s.then_inc(use_done if h else inverted, 1)
                dve.wait_ge(use_done, r + 1)

            def pair(i, odd):
                for kb, kind, tile in events(i):
                    r, which = use(i, kb, kind, tile)
                    if kind == "max" and kb <= LAST:
                        maximum(i + 1, AHEAD + 2 * kb + tile, r, which)
                        if kb == LAST and tile == 1:
                            split(i + 1, r)
                    elif kind == "max":
                        maximum(i + 2, 2 * (kb - LAST - 1) + tile, r, which)
                    elif kind == "turn":
                        take_turned(i + 1)
                    else:
                        normalize(i - 1, r, which)

            v.memset(mparts[:], 0.0).then_inc(m_zeroed, 1)
            dve.wait_ge(m_zeroed, 1)
            for r in range(2 * NT):
                maximum(0, r, r, r % 2)
            split(0, 2 * NT - 1)
            take_turned(0)
            for n in range(AHEAD):
                maximum(1, n, 2 * NT + 1 + n, (2 * NT + 1 + n) % 2)
            for i in range(NPAIR):
                pair(i, i % 2)
            normalize(NPAIR - 1, start[NPAIR], start[NPAIR] % 2)

        @block.tensor
        def _(pe):
            mm = nc.tensor

            def head(x, rows, n, a, b_):
                return x[0:rows, n, a:b_]

            def scores(i, kb):
                if i == kb == 0:
                    pe.wait_ge(consts, 16 * NCONST)
                if kb == 0:
                    pe.wait_ge(m_loaded, 48 * i + 48)
                for h in range(2):
                    for half in range(2):
                        at = (i * NT + kb) * 4 + 2 * h + half
                        if at >= 3:
                            pe.wait_ge(exp_done, at - 2)
                        mm.matmul(psS[at % 3][:], head(k, A_ROWS, i * 2 + h, kb * P, (kb + 1) * P),
                                  head(q, A_ROWS, i * 2 + h, half * 512, half * 512 + 512),
                                  start=True, stop=True).then_inc(s_ready, 1)
                        if half == 1:
                            yield

            def max_scores(p, tile, r, which):
                if tile == 0:
                    pe.wait_ge(loaded, NLOAD * (1 if 2 * p < FIRST else 2 if 2 * p < HA else 3))
                if r >= 2:
                    pe.wait_ge(use_done, r - 1)
                n, qb = p * 2 + tile // NT, tile % NT
                for half in range(2):
                    s = mm.matmul(psM[which][:, half * 512:half * 512 + 512], head(q, A_QK, n, qb * P, (qb + 1) * P),
                                  head(k, A_QK, n, half * 512, half * 512 + 512), start=True, stop=True)
                s.then_inc(use_ready, 1)

            def turn_max(p):
                r, which = use_of_turn(p)
                if p == 0:
                    pe.wait_ge(consts, 16 * NCONST)
                pe.wait_ge(m_split, 4 * p + 4)
                pe.wait_ge(use_done, r - 1)
                mm.transpose(psM[which][:, 0:P // 2].bitcast(BF16),
                             mparts[:].rearrange("p s t -> p (s t)"), t["identb"][:]).then_inc(use_ready, 1)

            def turn_out(i, r, which):
                pe.wait_ge(oT_ready, i + 1)
                pe.wait_ge(use_done, r - 1)
                for qc in range(NT // 2):
                    s = mm.transpose(psM[which][:, qc * P:(qc + 1) * P], oT[:, qc * P:(qc + 1) * P], t["identf"][:])
                s.then_inc(use_ready, 1)

            def values(i, kb, odd):
                at = i * NT + kb
                pe.wait_ge(exp_done, at * 4 + 4)
                pe.wait_ge(near_done, at + 1)
                if kb == 0:
                    pe.wait_ge(v_staged, i + 1)
                    if i > 0:
                        pe.wait_ge(oT_ready, i)
                for h in range(2):
                    for half in range(2):
                        c4 = 2 * h + half
                        s = mm.matmul(psO[c4 * VW:(c4 + 1) * VW, :], vst[:, odd, kb, h, :],
                                      prob[:, kb % 4, h, half * 512:half * 512 + 512],
                                      start=(kb == 0), stop=(kb == NT - 1), skip_group_check=True)
                s.then_inc(pv_done, 1)

            def pair(i, odd):
                these = events(i)
                for kb in range(NT):
                    todo = [e for e in these if e[0] == kb]
                    steps = scores(i, kb)
                    for n in range(2):
                        next(steps)
                        for e in todo[n:] if n else todo[:1]:
                            r, which = use(i, *e)
                            if e[1] == "max" and kb <= LAST:
                                max_scores(i + 1, AHEAD + 2 * kb + e[2], r, which)
                            elif e[1] == "max":
                                max_scores(i + 2, 2 * (kb - LAST - 1) + e[2], r, which)
                            elif e[1] == "turn":
                                turn_max(i + 1)
                            else:
                                turn_out(i - 1, r, which)
                    if kb >= 2:
                        values(i, kb - 2, odd)
                    elif i > 0:
                        values(i - 1, kb + NT - 2, 1 - odd)

            for r in range(2 * NT):
                max_scores(0, r, r, r % 2)
            turn_max(0)
            for n in range(AHEAD):
                max_scores(1, n, 2 * NT + 1 + n, (2 * NT + 1 + n) % 2)
            for i in range(NPAIR):
                pair(i, i % 2)
            values(NPAIR - 1, NT - 2, 1)
            values(NPAIR - 1, NT - 1, 1)
            turn_out(NPAIR - 1, start[NPAIR], start[NPAIR] % 2)


A_SEMS = ("consts loaded s_ready exp_done near_done pv_done use_ready use_done m_split m_loaded v_zeroed "
          "m_zeroed v_staged oT_ready inverted").split()


def attention_a(nc, t, d):
    with ExitStack() as c:
        t["sems_a"] = {n: c.enter_context(nc.semaphore("aa_" + n)) for n in A_SEMS}
        with nc.Fori(0, B // 2) as g:
            attend_a(nc, t, d, g)
            restart(nc, t["sems_a"])


HALF = HB // 2
B_BIAS = 3
B_BLOCK = 3 * NT
B_M = DB + B_BIAS + B_BLOCK
B_ROWS = B_M + 3
UNITS = NT * (NT + 1) // 2 * P // 512
BLOCKS = [(q, kb) for q in range(NT) for kb in range(q + 1)]
MAX_TILES = [[(7, 0)], [(6, 0)], [(5, 0)], [(4, 0)], [(3, 0), (2, 512)], [(1, 0), (0, 256)]]
USES = len(MAX_TILES) + 1
NULL_COL = 512
T_P1, T_P1B, T_P2, T_M = 0, 32, 64, 96
RING = 6
LAG = 3
LO_POOL = (0, 1, 5, 7)
B_SEMS = ("rows proj q_sq k_sq summed rooted rn q_normed k_normed q_scaled q_hi k_hi v_hi "
          "q_lo k_lo v_lo qa_turned ka_turned kb_turned qa_done ka_done kb_done copied "
          "m_loaded use_ready use_done s_ready exp_done null_sub null_exp null_parts nm_ready nm_chain pool_chain lo_dve lo_pool pv_done "
          "o_ready o_inverted o_done turned_out out_copied out_ready out_added").split()


B_WEIGHTS = ("wq", "wk", "wv", "wout", "norm_g", "norm_b", "identh", "upper", "lower")


def weights_b(nc, c):
    def sb(n, s, dt): return c.enter_context(nc.sbuf_tensor("wb_" + n, s, dt))
    return {"wq": sb("wq", [P, HB * DB], F32), "wk": sb("wk", [P, HB * DB], F32), "wv": sb("wv", [P, HB * DB], F32),
            "wout": sb("wout", [P, HB * DB // P, D], F32), "norm_g": sb("norm_g", [P, 1], F32),
            "norm_b": sb("norm_b", [P, 1], F32), "identh": sb("identh", [P, P], F16),
            "upper": sb("upper", [P, P], BF16), "lower": sb("lower", [P, P], BF16)}


def tiles_b(nc, c):
    def sb(n, s, dt): return c.enter_context(nc.sbuf_tensor("tb_" + n, s, dt))
    return {
        "c": sb("c", [P, DB], F32),
        "null_a": sb("null_a", [P, HB, NNULL], F16), "null_b": sb("null_b", [B_M, HB, NNULL], F16),
        "null_v": sb("null_v", [T_M, HB, NT, DB + 1], F16),
        "null_ah": sb("null_ah", [P, HALF, NNULL], F16), "null_bh": sb("null_bh", [B_M, HALF, NNULL], F16),
        "null_vh": sb("null_vh", [T_M, HALF, NT, DB + 1], F16),
        "xlT": sb("xlT", [P, L], F32), "xqT": sb("xqT", [P, L], F32),
        "qa": sb("qa", [P, HALF, L], F16), "ka": sb("ka", [P, HALF, L], F16),
        "qb": sb("qb", [B_ROWS, HALF, L], F16), "kb": sb("kb", [B_ROWS, HALF, L], F16),
        "kc": sb("kc", [B_M, HALF, L], F16),
        "v1": sb("v1", [P, NT, HALF, DB + 1], F16), "v2": sb("v2", [P, NT, HALF, DB], F16),
        "norm_sems": {n: c.enter_context(nc.semaphore("bn_" + n)) for n in ("dve", "var", "std", "pe", "pad")},
        "sems": {n: c.enter_context(nc.semaphore("b_" + n)) for n in B_SEMS},
    }


def load_b(nc, t, d):
    s = t["norm_sems"]
    with ExitStack() as c:
        def sb(n, s, dt): return c.enter_context(nc.sbuf_tensor("lb_" + n, s, dt))
        ks = sb("ks", [P, DB], F32)
        nk = sb("nk", [P, HB, NNULL], F32)
        sq = sb("sq", [P, HB, NNULL], F32)
        root = sb("root", [P, HB, NNULL], F32)
        halves = sb("halves", [P, P], F32)
        nv = sb("nv", [T_M, HB, DB + 1], F32)
        nvp = sb("nvp", [T_M, HB, DB + 1], F16)
        diag = sb("diag", [T_M, NT], F32)
        psN = c.enter_context(nc.psum_tensor("lb_psN", [P, 512], F32))
        landed, step, rooted, summed = (c.enter_context(nc.semaphore("lb_" + n)) for n in ("landed", "step", "root", "sum"))
        n_dma = 7 + HALF
        block = c.enter_context(nc.Block())

        @block.sync
        def _(sp):
            sp.dma_start(t["c"][:], d["q_scale"].broadcast_to([P, DB])).then_inc(landed, 16)
            sp.dma_start(ks[:], d["k_scale"].broadcast_to([P, DB])).then_inc(landed, 16)
            for i in range(2):
                sp.dma_start(nk[i * DB:(i + 1) * DB], d["null_k"]).then_inc(landed, 16)
            sp.dma_start(diag[:], d["b_diag"]).then_inc(landed, 16)
            sp.dma_start(t["null_b"][DB:B_M], d["b_nrows"]).then_inc(landed, 16)
            sp.dma_start(nv[:, :, 0:DB], d["null_v"]).then_inc(landed, 16)
            for n in range(HALF):
                sp.dma_start(t["qb"][DB:B_M, n, :], d["b_qrows"]).then_inc(landed, 16)
            sp.wait_ge(landed, 16 * n_dma)

        @block.tensor
        def _(pe):
            pe.wait_ge(step, 5)
            nc.tensor.matmul(psN[:, 0:HB * NNULL], halves[:], sq[:].rearrange("p h n -> p (h n)"),
                             start=True, stop=True).then_inc(summed, 1)

        @block.scalar
        def _(act):
            act.wait_ge(summed, 1)
            nc.scalar.activation(root[:], psN[:, 0:HB * NNULL].rearrange("p (h n) -> p h n", n=NNULL), ACT.Sqrt)\
              .then_inc(rooted, 1)

        @block.vector
        def _(dve):
            v = nc.vector
            st = Steps(step, 0)

            def run(ins):
                dve.wait_ge(step, st.after(ins))

            run(v.memset(halves[:], 0.5))
            run(v.memset(t["v1"][:, :, :, DB:DB + 1], 1.0))
            run(v.memset(nv[:, :, DB:DB + 1], 1.0))
            dve.wait_ge(landed, 16 * n_dma)
            run(v.scalar_tensor_tensor(out=t["c"][:], in0=t["c"][:], scalar=8.0, in1=ks[:], op0=ALU.mult, op1=ALU.mult))
            run(v.tensor_tensor(sq[:], nk[:], nk[:], ALU.mult))
            run(v.tensor_copy(nvp[:], nv[:]))
            lo = slice(T_P1B, T_P2)
            run(v.tensor_tensor(nvp[lo], nv[lo], nvp[lo], ALU.subtract))
            for i in range(NT):
                run(v.tensor_scalar(t["null_v"][:, :, i, :], nvp[:], diag[:, i:i + 1], None, ALU.mult))
            dve.wait_ge(rooted, 1)
            run(v.tensor_scalar(root[:], root[:], 1e-12, None, ALU.max))
            run(v.reciprocal(root[:], root[:]))
            run(v.tensor_tensor(nk[:], nk[:], root[:], ALU.mult))
            run(v.tensor_copy(t["null_a"][:], nk[:]))
            run(v.tensor_tensor(t["null_b"][0:DB], nk[0:DB], t["null_a"][0:DB], ALU.subtract))


def norm_b(nc, t, b):
    s = t["norm_sems"]
    with ExitStack() as c:
        def sb(n, s, dt): return c.enter_context(nc.sbuf_tensor("nb_" + n, s, dt))
        w = norm_buffers(sb, "ln", s["pad"])
        xl = sb("xl", [P, NT, D], F32)
        xq = sb("xq", [P, NT, D], F32)
        psT = [c.enter_context(nc.psum_tensor(f"nb_psT{i}", [P, L], F32)) for i in range(2)]
        n_dve = 8
        with nc.Block() as block:
            @block.vector
            def _(dve):
                st = Steps(s["dve"], b * n_dve)
                ins = layer_norm(nc.vector, dve, st, s["dve"],
                                 lambda i: t["x"][:, ds(b, 1), i, :].rearrange("p o e -> p (o e)"),
                                 xl, w, s["std"], b * 2 + 1, s["var"])
                dve.wait_ge(s["dve"], st.after(ins))
                ins = layer_norm(nc.vector, dve, st, s["dve"], lambda i: xl[:, i, :], xq, w, s["std"], b * 2 + 2, s["var"])
                dve.wait_ge(s["dve"], st.after(ins))
                dve.sem_inc(w["pad"], 1)
                assert st.n == n_dve

            @block.scalar
            def _(act):
                for i in range(2):
                    act.wait_ge(s["var"], b * 2 + i + 1)
                    nc.scalar.activation(w["std"][:], w["var"][:], ACT.Sqrt).then_inc(s["std"], 1)
                act.wait_ge(s["pe"], b * 2 + 1)
                nc.scalar.activation(t["xlT"][:], psT[0][:], ACT.Copy)
                act.wait_ge(s["pe"], b * 2 + 2)
                nc.scalar.activation(t["xqT"][:], psT[1][:], ACT.Identity, bias=t["norm_b"][:, 0:1],
                                     scale=t["norm_g"][:, 0:1])

            @block.tensor
            def _(pe):
                for j, x in enumerate((xl, xq)):
                    pe.wait_ge(s["dve"], b * n_dve + 4 * j + 4)
                    for i in range(NT):
                        ins = nc.tensor.transpose(psT[j][:, i * P:(i + 1) * P], x[:, i, :], t["identf"][:])
                    ins.then_inc(s["pe"], 1)


def project_b(nc, t, d, hf):
    s = t["sems"]
    W = HALF * DB
    with ExitStack() as c:
        def sb(n, s, dt): return c.enter_context(nc.sbuf_tensor("pb_" + n, s, dt))
        sq = t["o_b"][:, 0:4, :].rearrange("p (i j) (h e) -> p i j h e", j=2, e=DB)
        ss = sb("ss", [P, 2, 2, HALF], F32)
        root = sb("root", [P, 2, 2, HALF], F32)
        rn = sb("rn", [P, 2, 2, HALF], F32)
        qn = sb("qn", [P, 2, HALF, DB], F32)
        kn = sb("kn", [P, 2, HALF, DB], F32)
        qc = sb("qc", [P, 2, HALF, DB], F32)
        qp = sb("qp", [P, 2, HALF, 2, DB], F16)
        kp = sb("kp", [P, 2, HALF, 3, DB], F16)
        ps = [[c.enter_context(nc.psum_tensor(f"pb_ps{n}{i}", [P, HALF, DB], F32)) for i in range(2)] for n in "qkv"]
        psX = [c.enter_context(nc.psum_tensor(f"pb_psX{i}", [P, HALF, P], F16)) for i in range(2)]

        with nc.Block() as block:
            @block.sync
            def _(sp):
                rows = d["b_krows"][ds(hf, 1), :, :, :].rearrange("o r h k -> r (o h) k")
                sp.dma_start(t["kb"][DB:B_ROWS, :, :], rows).then_inc(s["rows"], 16)
                sp.dma_start(t["kc"][DB:B_M, :, :], rows[0:B_M - DB]).then_inc(s["rows"], 16)
                for n in ("null_a", "null_b", "null_v"):
                    sp.dma_start(t[n + "h"][:], t[n][:, ds(hf * HALF, HALF)]).then_inc(s["rows"], 16)
                for i in range(4):
                    cols = slice(i * 2 * P, (i + 1) * 2 * P)
                    sp.wait_ge(s["qa_done"], 2 * i + 2)
                    sp.dma_start(t["qb"][0:DB, :, cols], t["qa"][0:DB, :, cols]).then_inc(s["rows"], 16)
                    sp.wait_ge(s["ka_done"], 2 * i + 2)
                    sp.dma_start(t["kc"][0:DB, :, cols], t["ka"][0:DB, :, cols]).then_inc(s["rows"], 16)
                sp.wait_ge(s["rows"], 16 * 13)

            @block.tensor
            def _(pe):
                m = nc.tensor
                def project(i):
                    for j, (x, w, done) in enumerate((("xqT", "wq", "q_normed"), ("xlT", "wk", "k_normed"),
                                                      ("xlT", "wv", "v_lo"))):
                        if i >= 2:
                            pe.wait_ge(s[done], i - 1)
                        m.matmul(ps[j][i % 2][:].rearrange("p h e -> p (h e)"), t[x][:, i * P:(i + 1) * P],
                                 t[w][:, ds(hf * W, W)], start=True, stop=True).then_inc(s["proj"], 1)

                project(0)
                for i in range(NT + 2):
                    if i + 1 < NT:
                        project(i + 1)
                    if i >= 2:
                        k = i - 2
                        for j, (part, turned) in enumerate((("q_lo", "qa_turned"), ("k_lo", "ka_turned"),
                                                            (None, "kb_turned"))):
                            if part:
                                pe.wait_ge(s[part], k + 1)
                            if j == 2:
                                pe.wait_ge(s["qa_done"], k + 1)
                            elif k > 0:
                                pe.wait_ge(s[("ka_done", "kb_done")[j]], k)
                            if j == 1:
                                pe.wait_ge(s["copied"], k + 1)
                            for n in range(HALF):
                                src = qp[:, k % 2, n, :, :] if j == 0 else kp[:, k % 2, n, 2 - j:4 - j, :]
                                ins = m.transpose(psX[(3 * k + j) % 2][:, n, :], src.rearrange("p s e -> p (s e)"),
                                                  t["identh"][:])
                            ins.then_inc(s[turned], 1)

            @block.scalar
            def _(act):
                a = nc.scalar
                for i in range(NT + 2):
                    if i < NT:
                        for j, name in enumerate(("q_sq", "k_sq")):
                            act.wait_ge(s["proj"], i * 3 + j + 1)
                            if i >= 2:
                                act.wait_ge(s["summed"], (i - 2) * 2 + j + 1)
                            a.activation(sq[:, i % 2, j], ps[j][i % 2][:], ACT.Square).then_inc(s[name], 1)
                        act.wait_ge(s["proj"], i * 3 + 3)
                        a.activation(t["v1"][:, i, :, 0:DB], ps[2][i % 2][:], ACT.Copy).then_inc(s["v_hi"], 1)
                    if 1 <= i <= NT:
                        k = i - 1
                        act.wait_ge(s["k_normed"], k + 1)
                        if k >= 2:
                            act.wait_ge(s["kb_turned"], k - 1)
                        a.activation(kp[:, k % 2, :, 1, :], kn[:, k % 2], ACT.Copy).then_inc(s["k_hi"], 1)
                        act.wait_ge(s["q_scaled"], k + 1)
                        if k >= 2:
                            act.wait_ge(s["qa_turned"], k - 1)
                        a.activation(qp[:, k % 2, :, 0, :], qc[:, k % 2], ACT.Copy).then_inc(s["q_hi"], 1)
                    if i < NT:
                        act.wait_ge(s["summed"], i * 2 + 2)
                        a.activation(root[:, i % 2], ss[:, i % 2], ACT.Sqrt).then_inc(s["rooted"], 1)
                    if i >= 2:
                        k = i - 2
                        for j, (n, turned, done) in enumerate((("qa", "qa_turned", "qa_done"), ("ka", "ka_turned", "ka_done"))):
                            act.wait_ge(s[turned], k + 1)
                            a.activation(t[n][:, :, k * P:(k + 1) * P], psX[(3 * k + j) % 2][:], ACT.Copy)\
                             .then_inc(s[done], 1)

            @block.gpsimd
            def _(pool):
                g = nc.gpsimd
                for i in range(NT + 1):
                    if i >= 1:
                        k = i - 1
                        pool.wait_ge(s["k_hi"], k + 1)
                        g.tensor_tensor(kp[:, k % 2, :, 0, :], kn[:, k % 2], kp[:, k % 2, :, 1, :], ALU.subtract)\
                         .then_inc(s["k_lo"], 1)
                        pool.wait_ge(s["q_hi"], k + 1)
                        g.tensor_tensor(qp[:, k % 2, :, 1, :], qc[:, k % 2], qp[:, k % 2, :, 0, :], ALU.subtract)\
                         .then_inc(s["q_lo"], 1)
                    if i < NT:
                        pool.wait_ge(s["q_normed"], i + 1)
                        if i >= 2:
                            pool.wait_ge(s["q_lo"], i - 1)
                        g.tensor_tensor(qc[:, i % 2], qn[:, i % 2], t["c"][:].unsqueeze(1).broadcast_to([P, HALF, DB]),
                                        ALU.mult).then_inc(s["q_scaled"], 1)

            @block.vector
            def _(dve):
                v = nc.vector
                for i in range(NT + 2):
                    if i < NT:
                        for j, name in enumerate(("q_sq", "k_sq")):
                            dve.wait_ge(s[name], i + 1)
                            v.tensor_reduce(ss[:, i % 2, j], sq[:, i % 2, j], AX.X, ALU.add).then_inc(s["summed"], 1)
                        dve.wait_ge(s["v_hi"], i + 1)
                        v.tensor_tensor(t["v2"][:, i], ps[2][i % 2][:], t["v1"][:, i, :, 0:DB], ALU.subtract)\
                         .then_inc(s["v_lo"], 1)
                    if 1 <= i <= NT:
                        k = i - 1
                        dve.wait_ge(s["k_hi"], k + 1)
                        v.tensor_copy(kp[:, k % 2, :, 2, :], kp[:, k % 2, :, 1, :]).then_inc(s["copied"], 1)
                    if i < NT:
                        dve.wait_ge(s["rooted"], i + 1)
                        v.tensor_scalar(root[:, i % 2], root[:, i % 2], 1e-12, None, ALU.max).then_inc(s["rn"], 1)
                        dve.wait_ge(s["rn"], i * 2 + 1)
                        v.reciprocal(rn[:, i % 2], root[:, i % 2]).then_inc(s["rn"], 1)
                        dve.wait_ge(s["rn"], i * 2 + 2)
                        for j, (to, name) in enumerate(((qn, "q_normed"), (kn, "k_normed"))):
                            if j == 0 and i >= 2:
                                dve.wait_ge(s["q_scaled"], i - 1)
                            if j == 1 and i >= 2:
                                dve.wait_ge(s["k_lo"], i - 1)
                            v.tensor_tensor(to[:, i % 2], ps[j][i % 2][:],
                                            rn[:, i % 2, j].unsqueeze(2).broadcast_to([P, HALF, DB]), ALU.mult)\
                             .then_inc(s[name], 1)
                    if i >= 2:
                        k = i - 2
                        dve.wait_ge(s["kb_turned"], k + 1)
                        v.tensor_copy(t["kb"][0:DB, :, k * P:(k + 1) * P], psX[(3 * k + 2) % 2][0:DB])\
                         .then_inc(s["kb_done"], 1)


def attend_b(nc, t):
    s = t["sems"]
    with ExitStack() as c:
        def sb(n, s, dt): return c.enter_context(nc.sbuf_tensor("ab_" + n, s, dt))
        def ps(n, s, dt): return c.enter_context(nc.psum_tensor("ab_" + n, s, dt))
        hi = sb("hi", [P, RING, 512], F16)
        lo = sb("lo", [P, RING, 512], F16)
        full = sb("full", [P, RING, 512], F32)
        nm = sb("nm", [P, NT], F32)
        rest = sb("rest", [P, NT], F32)
        null = sb("null", [P, NT, NNULL], F32)
        nullx = sb("nullx", [P, NT, NNULL], F32)
        nullp = sb("nullp", [P, NT * NNULL], F32)
        nmax = sb("nmax", [P, NT], F32)
        turn = sb("turn", [P, P], F16)
        turned = sb("turned", [P, P], F16)
        rsum = sb("rsum", [P, NT], F32)
        warm = sb("warm", [P, 1], F32)
        psS = [ps(f"psS{i}", [P, 512], F32) for i in range(2)]
        psM = [ps(f"psM{i}", [P, L], F32) for i in range(2)]
        psO = [ps(f"psO{i}", [P, 512], F32) for i in range(2)]
        LO_DVE = [u for u in range(UNITS) if u not in LO_POOL]

        def unit(n, u):
            return n * UNITS + u

        def use(n, k):
            return n * USES + k

        SPLIT = 2
        EARLY = {6: [0], 7: [1], 8: [2]}
        LATE = {0: [3, 4], 1: [5], 5: [6]}

        def ahead(n, u):
            now = [(n + 1, k) for k in LATE.get(u, [])] + [(n + 2, k) for k in EARLY.get(u, [])]
            return [(m, k) for m, k in now if m < HALF]

        first = [(0, k) for k in range(USES)] + [(1, k) for u in sorted(EARLY) for k in EARLY[u]]

        with nc.Block() as block:
            @block.tensor
            def _(pe):
                m = nc.tensor

                def row(x, rows, n, a, b):
                    return t[x][0:rows, n, a:b]

                def scores(n, par, u):
                    if u == 0:
                        pe.wait_ge(s["m_loaded"], n * 48 + 48)
                    if unit(n, u) >= 2:
                        pe.wait_ge(s["exp_done"], unit(n, u) * 2 - 2)
                    S = psS[(par + u) % 2]
                    for i, (q, kb) in enumerate(BLOCKS[4 * u:4 * u + 4]):
                        out = S[:, i * P:(i + 1) * P]
                        keys, queries = (kb * P, kb * P + P), (q * P, q * P + P)
                        m.matmul(out, row("ka", P, n, *keys), row("qa", P, n, *queries), start=True, stop=False)
                        ins = m.matmul(out, row("kb", B_ROWS, n, *keys), row("qb", B_ROWS, n, *queries),
                                       start=False, stop=(q != kb))
                        if q == kb:
                            ins = m.matmul(out, t["identb"][:], t["lower"][:], start=False, stop=True)
                    ins.then_inc(s["s_ready"], 1)

                def max_tile(n, par, k):
                    M = psM[(par + k) % 2]
                    if use(n, k) >= 2:
                        pe.wait_ge(s["use_done"], use(n, k) - 1)
                    if k == USES - 1:
                        pe.wait_ge(s["null_parts"], n + 1)
                        m.transpose(M[:, 0:P // 2].bitcast(F16), turn[:], t["identh"][:]).then_inc(s["use_ready"], 1)
                        return
                    for q, col in MAX_TILES[k]:
                        end = (q + 1) * P
                        for a in range(0, end, 512):
                            z = min(end, a + 512)
                            ins = m.matmul(M[:, col + a:col + z], row("qb", B_M, n, q * P, q * P + P),
                                           row("kc", B_M, n, a, z), start=True, stop=(z < end))
                        ins = m.matmul(M[:, col + q * P:col + end], t["identb"][:], t["upper"][:], start=False, stop=True)
                    if k == USES - 2:
                        for q in range(NT):
                            out = M[:, NULL_COL + q * NNULL:NULL_COL + (q + 1) * NNULL]
                            m.matmul(out, row("qa", P, n, q * P, q * P + P),
                                     t["null_ah"][:, n, :], start=True, stop=False)
                            ins = m.matmul(out, row("qb", B_M, n, q * P, q * P + P),
                                           t["null_bh"][:, n, :], start=False, stop=True)
                    ins.then_inc(s["use_ready"], 1)

                def values(n, par, u):
                    for half, first in ((0, 0), (1, 2)):
                        if u == first:
                            if n > 0:
                                pe.wait_ge(s["o_done"], n * 2 + half - 1)
                            pe.wait_ge(s["use_done"], use(n, USES - 1) + 1)
                            nv = t["null_vh"][:, n, half * 4:half * 4 + 4, :]
                            m.matmul(psO[half][:, 0:4 * (DB + 1)], turned[0:T_M, :], nv.rearrange("p t e -> p (t e)"),
                                     start=True, stop=False, skip_group_check=True)
                    pe.wait_ge(s["exp_done"], unit(n, u) * 2 + 2)
                    if u in LO_POOL:
                        pe.wait_ge(s["lo_pool"], n * len(LO_POOL) + LO_POOL.index(u) + 1)
                    else:
                        pe.wait_ge(s["lo_dve"], n * len(LO_DVE) + LO_DVE.index(u) + 1)
                    r = (3 * par + u) % RING
                    for i, (q, kb) in enumerate(BLOCKS[4 * u:4 * u + 4]):
                        out = psO[q // 4][:, q % 4 * (DB + 1):(q % 4 + 1) * (DB + 1)]
                        v1, v2 = t["v1"][:, kb, n, :], t["v2"][:, kb, n, :]
                        cols = slice(i * P, (i + 1) * P)
                        m.matmul(out, hi[:, r, cols], v1, start=False, stop=False, skip_group_check=True)
                        m.matmul(out[:, 0:DB], hi[:, r, cols], v2, start=False, stop=False, skip_group_check=True)
                        ins = m.matmul(out, lo[:, r, cols], v1, start=False, stop=(q == kb), skip_group_check=True)
                        if q == kb and q % 4 == 3:
                            ins.then_inc(s["o_ready"], 1)
                    if u == UNITS - 1:
                        pe.sem_inc(s["pv_done"], 1)
                    else:
                        ins.then_inc(s["pv_done"], 1)

                def head(n, par):
                    for u in range(UNITS):
                        scores(n, par, u)
                        for h, k in ahead(n, u):
                            max_tile(h, h % 2, k)
                        if u >= LAG:
                            values(n, par, u - LAG)
                        elif n > 0:
                            values(n - 1, 1 - par, u - LAG + UNITS)

                for h, k in first:
                    max_tile(h, h % 2, k)
                for n in range(HALF):
                    head(n, n % 2)
                for u in range(UNITS - LAG, UNITS):
                    values(HALF - 1, 1, u)

            @block.sync
            def _(sp):
                def store_max(n):
                    sp.wait_ge(s["use_done"], use(n, USES - 1) + 1)
                    for i in range(3):
                        to = t["qb"][B_M + i:B_M + i + 1, ds(n, 1), :].rearrange("r o (q e) -> r (o q) e", e=P)
                        sp.dma_start(to, turned[T_M + i * NT:T_M + (i + 1) * NT, :]).then_inc(s["m_loaded"], 16)
                    sp.wait_ge(s["m_loaded"], n * 48 + 48)

                for n in range(HALF):
                    store_max(n)

            @block.scalar
            def _(act):
                a = nc.scalar
                a.activation(warm[:], t["identf"][:, 0:1], ACT.Exp)

                def exp_null(n):
                    act.wait_ge(s["null_sub"], n + 1)
                    a.activation(nullp[:], nullx[:].rearrange("p t n -> p (t n)"), ACT.Exp).then_inc(s["null_exp"], 1)

                def head(n, par):
                    for u in range(UNITS):
                        act.wait_ge(s["s_ready"], unit(n, u) + 1)
                        if unit(n, u) >= RING:
                            act.wait_ge(s["pv_done"], unit(n, u) - RING + 1)
                        r = (3 * par + u) % RING
                        for to in (hi, full):
                            a.activation(to[:, r, :], psS[(par + u) % 2][:], ACT.Exp).then_inc(s["exp_done"], 1)
                        if u == 2 and n < HALF - 1:
                            exp_null(n + 1)

                exp_null(0)
                for n in range(HALF):
                    head(n, n % 2)

            @block.gpsimd
            def _(pool):
                p = nc.gpsimd
                p.memset(turn[:], 0.0).then_inc(s["pool_chain"], 1)

                def maximum(n):
                    base = n * 6 + 1
                    step = [0]

                    def run(ins):
                        ins.then_inc(s["pool_chain"], 1)
                        step[0] += 1
                        pool.wait_ge(s["pool_chain"], base + step[0])

                    pool.wait_ge(s["nm_ready"], n + 1)
                    pool.wait_ge(s["pool_chain"], base)
                    if n > 0:
                        pool.wait_ge(s["null_parts"], n)
                    p.tensor_tensor(nullx[:], null[:], nm[:].unsqueeze(2).broadcast_to([P, NT, NNULL]), ALU.add)\
                     .then_inc(s["null_sub"], 1)
                    m1, m2, m3 = (turn[:, T_M + i * NT:T_M + (i + 1) * NT] for i in range(3))
                    run(p.tensor_copy(m1, nm[:]))
                    run(p.tensor_tensor(rest[:], nm[:], m1, ALU.subtract))
                    run(p.tensor_copy(m2, rest[:]))
                    run(p.tensor_tensor(m3, rest[:], m2, ALU.subtract))
                    pool.wait_ge(s["null_exp"], n + 1)
                    w = NT * NNULL
                    run(p.tensor_copy(turn[:, T_P1:T_P1 + w], nullp[:]))
                    run(p.tensor_copy(turn[:, T_P1B:T_P1B + w], turn[:, T_P1:T_P1 + w]))
                    p.tensor_tensor(turn[:, T_P2:T_P2 + w], nullp[:], turn[:, T_P1:T_P1 + w], ALU.subtract)\
                     .then_inc(s["null_parts"], 1)

                def head(n, par):
                    for i, u in enumerate(LO_POOL):
                        if i == SPLIT and n < HALF - 1:
                            maximum(n + 1)
                        pool.wait_ge(s["exp_done"], unit(n, u) * 2 + 2)
                        r = (3 * par + u) % RING
                        p.tensor_tensor(lo[:, r, :], full[:, r, :], hi[:, r, :], ALU.subtract).then_inc(s["lo_pool"], 1)

                maximum(0)
                for n in range(HALF):
                    head(n, n % 2)

            @block.vector
            def _(dve):
                v = nc.vector

                def max_tile(n, par, k):
                    M = psM[(par + k) % 2]
                    dve.wait_ge(s["use_ready"], use(n, k) + 1)
                    if k == USES - 1:
                        if n > 0:
                            dve.wait_ge(s["m_loaded"], n * 48)
                            dve.wait_ge(s["pv_done"], unit(n, 0) - UNITS + 3)
                        v.tensor_copy(turned[:], M[:, 0:P // 2].bitcast(F16)).then_inc(s["use_done"], 1)
                        return
                    if k == 0 and n > 0:
                        dve.wait_ge(s["null_parts"], n)
                    last = k == USES - 2
                    for i, (q, col) in enumerate(MAX_TILES[k]):
                        ins = v.tensor_reduce(nm[:, q:q + 1], M[:, col:col + (q + 1) * P], AX.X, ALU.max, negate=True)
                    if not last:
                        ins.then_inc(s["use_done"], 1)
                        return
                    ns = M[:, NULL_COL:NULL_COL + NT * NNULL].rearrange("p (t n) -> p t n", n=NNULL)
                    v.tensor_reduce(nmax[:], ns, AX.X, ALU.max, negate=True).then_inc(s["nm_chain"], 1)
                    v.tensor_copy(null[:], ns).then_inc(s["use_done"], 1)
                    dve.wait_ge(s["nm_chain"], n + 1)
                    dve.wait_ge(s["use_done"], use(n, k) + 1)
                    v.tensor_tensor(nm[:], nm[:], nmax[:], ALU.min).then_inc(s["nm_ready"], 1)

                def divide(n, half):
                    o = psO[half][:, 0:4 * (DB + 1)].rearrange("p (t e) -> p t e", e=DB + 1)
                    dve.wait_ge(s["o_ready"], n * 2 + half + 1)
                    r = rsum[:, half * 4:half * 4 + 4]
                    v.reciprocal(r, o[:, :, DB]).then_inc(s["o_inverted"], 1)
                    dve.wait_ge(s["o_inverted"], n * 2 + half + 1)
                    v.tensor_tensor(t["o_b"][:, half * 4:half * 4 + 4, ds(n * DB, DB)], o[:, :, 0:DB],
                                    r.unsqueeze(2).broadcast_to([P, 4, DB]), ALU.mult).then_inc(s["o_done"], 1)

                def head(n, par):
                    for u in range(UNITS):
                        for h, k in ahead(n, u):
                            max_tile(h, h % 2, k)
                        if u == 2 and n > 0:
                            divide(n - 1, 1)
                        if u == 5:
                            divide(n, 0)
                        if u not in LO_POOL:
                            dve.wait_ge(s["exp_done"], unit(n, u) * 2 + 2)
                            r = (3 * par + u) % RING
                            v.tensor_tensor(lo[:, r, :], full[:, r, :], hi[:, r, :], ALU.subtract).then_inc(s["lo_dve"], 1)

                for h, k in first:
                    max_tile(h, h % 2, k)
                for n in range(HALF):
                    head(n, n % 2)
                divide(HALF - 1, 1)


def out_b(nc, t, hf, b):
    s = t["sems"]
    C = HALF * DB // P
    with ExitStack() as c:
        oT = c.enter_context(nc.sbuf_tensor("ob_oT", [P, 2, C * P], F32))
        psT = [c.enter_context(nc.psum_tensor(f"ob_psT{i}", [P, C * P], F32)) for i in range(2)]
        psX = [c.enter_context(nc.psum_tensor(f"ob_psX{i}", [P, P], F32)) for i in range(2)]
        with nc.Block() as block:
            @block.tensor
            def _(pe):
                m = nc.tensor
                for i in range(NT + 1):
                    if i < NT:
                        if i >= 2:
                            pe.wait_ge(s["out_copied"], i - 1)
                        for j in range(C):
                            ins = m.transpose(psT[i % 2][:, j * P:(j + 1) * P], t["o_b"][:, i, j * P:(j + 1) * P],
                                              t["identf"][:])
                        ins.then_inc(s["turned_out"], 1)
                    if i >= 1:
                        k = i - 1
                        pe.wait_ge(s["out_copied"], k + 1)
                        if k >= 2:
                            pe.wait_ge(s["out_added"], k - 1)
                        for j in range(C):
                            w = t["wout"][:, ds(hf * C + j, 1), :].rearrange("p o e -> p (o e)")
                            ins = m.matmul(psX[k % 2][:], oT[:, k % 2, j * P:(j + 1) * P], w, start=(j == 0), stop=(j == C - 1))
                        ins.then_inc(s["out_ready"], 1)

            @block.scalar
            def _(act):
                for i in range(NT):
                    act.wait_ge(s["turned_out"], i + 1)
                    if i >= 2:
                        act.wait_ge(s["out_ready"], i - 1)
                    nc.scalar.activation(oT[:, i % 2, :], psT[i % 2][:], ACT.Copy).then_inc(s["out_copied"], 1)

            @block.vector
            def _(dve):
                for i in range(NT):
                    dve.wait_ge(s["out_ready"], i + 1)
                    x = t["x"][:, ds(b, 1), i, :].rearrange("p o e -> p (o e)")
                    nc.vector.tensor_tensor(x, x, psX[i % 2][:], ALU.add).then_inc(s["out_added"], 1)


def restart(nc, sems):
    numbers = sorted(s.num for s in sems.values())
    assert numbers == list(range(numbers[0], numbers[-1] + 1))
    with nc.Block() as block:
        @block.sync
        def _(sp):
            sp.sem_clear(range(numbers[0], numbers[-1] + 1))


def attention_b(nc, t, d):
    with nc.Fori(0, B) as b:
        norm_b(nc, t, b)
        with nc.Fori(0, 2) as hf:
            project_b(nc, t, d, hf)
            attend_b(nc, t)
            out_b(nc, t, hf, b)
            restart(nc, t["sems"])


def hybrid_layer(nc, d):
    def sb(c, n, s, dt): return c.enter_context(nc.sbuf_tensor(n, s, dt))
    d["parts"] = nc.dram_tensor("parts", (2 * B, 3, P, L), BF16, kind="Internal").ap()
    with ExitStack() as whole:
        t = {"identf": sb(whole, "identf", [P, P], F32), "identb": sb(whole, "identb", [P, P], BF16)}
        t["o_a"] = sb(whole, "o", [P, NT, B * HA, DA], F32)
        t["o_b"] = t["o_a"][:].rearrange("p t h e -> p t (h e)")
        with ExitStack() as c:
            t["v_a"] = sb(c, "v_a", [P, NT, B * HA, DA + 1], F32)
            project_a(nc, t, d)
            attention_a(nc, t, d)
        t["x"] = sb(whole, "x", [P, B, NT, D], F32)
        with ExitStack() as second:
            t.update(weights_b(nc, second))
            with ExitStack() as c:
                t.update(ffn_tiles(nc, c, "w1", True))
                ffn(nc, t, d, None, B_WEIGHTS, "f1", True)
            with ExitStack() as c:
                t.update(tiles_b(nc, c))
                load_b(nc, t, d)
                attention_b(nc, t, d)
        with ExitStack() as c:
            t.update(ffn_tiles(nc, c, "w2", False))
            ffn(nc, t, d, d["out"], (), "f2", False)



def sorted_positions():
    import numpy as np
    pos = (np.arange(L, dtype=np.float32) * np.float32((1.0 + np.sqrt(5.0)) / 2.0)) % np.float32(1.0)
    return pos, np.argsort(pos, kind="stable")


def parts_of(a, dtype, n):
    import numpy as np
    out, rest = [], np.asarray(a, np.float64)
    for _ in range(n):
        out.append(rest.astype(dtype))
        rest = rest - out[-1].astype(np.float64)
    return out


def constants():
    import numpy as np
    bf = np.dtype(mybir.dt.np(BF16))
    pos, order = sorted_positions()
    p = pos[order].astype(np.float64)
    block = np.arange(L) // P
    krows = np.zeros((A_ROWS - A_M, L), bf)
    qrows = np.zeros((A_ROWS - A_POS, L), bf)
    krows[0:3] = 1
    for r in range(NT):
        sign = np.sign(block - r).astype(np.float64)
        mid = p[block == r].mean()
        small = np.where(sign == 0, 0.0, np.log1p(1e-8 * np.exp(sign * (p - mid))))
        for s in range(3):
            krows[A_POS - A_M + 3 * r + s] = sign
            krows[A_KPOS - A_M + 3 * r + s] = parts_of(-sign * p + small, bf, 3)[s]
            qrows[3 * r + s] = np.where(block == r, parts_of(p, bf, 3)[s].astype(np.float64), 0.0)
            qrows[A_KPOS - A_POS + 3 * r + s] = block == r
    pb = p.reshape(NT, P)
    near = np.exp(-np.abs(pb[:, :, None] - pb[:, None, :])) + 1e-8
    perm = np.zeros((P, NT, L), bf)
    for i, tok in enumerate(order):
        perm[i % P, i // P, tok] = 1
    return {
        "a_krows": krows, "a_qrows": qrows,
        "near": np.ascontiguousarray(near.transpose(1, 0, 2)).astype(np.float32),
        "perm": perm, "identf": np.eye(P, dtype=np.float32), "identb": np.eye(P).astype(bf),
    }


def ffn_layout(w):
    import numpy as np
    c = np.ascontiguousarray
    return {
        "w1": c(w["W1"].T), "tw1": c(w["TW1"].transpose(2, 0, 1)),
        "w2": c(w["W2"].T.reshape(FB, P, D).transpose(1, 0, 2).reshape(P, FF)),
        "tw2": c(w["TW2"].transpose(2, 0, 1).reshape(FB, P, NE, D).transpose(1, 2, 0, 3).reshape(P, NE, FF)),
        "gw1": c(w["gate_w1"].T), "gb1": c(w["gate_b1"].reshape(P, 1)), "gw2": c(w["gate_w2"].T),
        "gb2row": c(w["gate_b2"].reshape(1, NE)), "gb2col": c(w["gate_b2"].reshape(NE, 1)),
        "b1": c(w["b1"].reshape(FB, P).T), "tb1": c(w["Tb1"].reshape(NE, FB, P).transpose(2, 1, 0)),
        "tb2": c(w["Tb2"]), "b2": c(w["b2"].reshape(1, D)),
    }


def constants_b():
    import numpy as np
    start = 2.0 ** (-2.0 ** (-(np.log2(HB) - 3)))
    slopes = np.array([start * start ** i for i in range(HB)], dtype=np.float32).astype(np.float64)
    key, block = np.arange(L), np.arange(L) // P
    krows = np.zeros((HB, B_ROWS - DB, L), np.float16)
    nrows = np.zeros((HB, B_M - DB, NNULL), np.float16)
    qrows = np.zeros((B_M - DB, L), np.float16)
    qrows[0:B_BIAS] = 1
    for h in range(HB):
        krows[h, 0:B_BIAS] = parts_of(slopes[h] * (key - P * block), np.float16, 3)
        nrows[h, 0:B_BIAS] = parts_of(slopes[h] * (np.arange(NNULL) - NNULL), np.float16, 3)
        for r in range(NT):
            at = slice(B_BIAS + 3 * r, B_BIAS + 3 * r + 3)
            krows[h, at] = parts_of(slopes[h] * P * (block - r), np.float16, 3)
            nrows[h, at] = parts_of(slopes[h] * P * (0 * np.arange(NNULL) - r), np.float16, 3)
            qrows[at] = block == r
    krows[:, B_M - DB:] = 1
    k, q = np.meshgrid(np.arange(P), np.arange(P), indexing="ij")
    diag = np.zeros((T_M, NT), np.float32)
    for first in (T_P1, T_P1B, T_P2):
        for i in range(NT):
            diag[first + NNULL * i:first + NNULL * (i + 1), i] = 1
    return {
        "b_krows": np.ascontiguousarray(krows.reshape(2, HALF, B_ROWS - DB, L).transpose(0, 2, 1, 3)),
        "b_nrows": np.ascontiguousarray(nrows.transpose(1, 0, 2)), "b_qrows": qrows, "b_diag": diag,
        "identh": np.eye(P, dtype=np.float16),
        "lower": np.where(k > q, -1e30, 0.0).astype(mybir.dt.np(BF16)),
        "upper": np.where(q > k, -1e30, 0.0).astype(mybir.dt.np(BF16)),
    }


def layout_b(w):
    import numpy as np
    c = np.ascontiguousarray
    null = w["null_kv"].reshape(HB, NNULL, 2, DB)
    null_v = np.zeros((T_M, HB, DB), np.float32)
    for first in (T_P1, T_P1B, T_P2):
        for i in range(NT):
            null_v[first + NNULL * i:first + NNULL * (i + 1)] = null[:, :, 1].transpose(1, 0, 2)
    return {
        "wq": c(w["Wq"]), "wk": c(w["Wkv"][:, :HB * DB]), "wv": c(w["Wkv"][:, HB * DB:]),
        "wout": c(w["Wout"].reshape(HB * DB // P, P, D).transpose(1, 0, 2)),
        "norm_g": c(w["norm_g"].reshape(D, 1)), "norm_b": c(w["norm_b"].reshape(D, 1)),
        "q_scale": c(w["q_scale"].reshape(1, DB)), "k_scale": c(w["k_scale"].reshape(1, DB)),
        "null_k": c(null[:, :, 0].transpose(2, 0, 1)), "null_v": null_v,
    }


def kernel(**inputs):
    import numpy as np
    import concourse.bacc as bacc
    from concourse.bass_utils import run_bass_kernel_spmd

    w = {n: np.asarray(a) for n, a in inputs.items()}
    a = {n.removeprefix("L0_attn_a_"): v for n, v in w.items() if n.startswith("L0_attn_a_")}
    b = {n.removeprefix("L0_attn_b_"): v for n, v in w.items() if n.startswith("L0_attn_b_")}
    f = {n.removeprefix("L0_ffn_"): v for n, v in w.items() if n.startswith("L0_ffn_")}
    order = sorted_positions()[1]
    arrays = {
        **constants(), **constants_b(), **layout_b(b), **ffn_layout(f),
        "x": a["x"], "x_sorted": np.ascontiguousarray(a["x"][:, order]), "w_qkv": a["w_qkv"],
        "wproj": a["w_proj"], "bproj": a["b_proj"].reshape(1, D), "ones": np.ones((1, P), np.float32),
    }
    nc = bacc.Bacc("TRN2", target_bir_lowering=False, num_devices=1)
    d = {n: nc.dram_tensor(f"in_{n}_dram", v.shape, mybir.dt.from_np(v.dtype), kind="ExternalInput").ap()
         for n, v in arrays.items()}
    d["out"] = nc.dram_tensor("out_0_dram", (B, L, D), F32, kind="ExternalOutput").ap()
    hybrid_layer(nc, d)
    r = run_bass_kernel_spmd(nc, [{f"in_{n}_dram": v for n, v in arrays.items()}], core_ids=[0])
    return r.results[0]["out_0_dram"]
```

```python
from contextlib import ExitStack

import concourse.bass as bass
from concourse import mybir

F32 = mybir.dt.float32
F16 = mybir.dt.float16
BF16 = mybir.dt.bfloat16
ALU = mybir.AluOpType
ACT = mybir.ActivationFunctionType
AX = mybir.AxisListType
ds = bass.ds

P = 128
B, L, D = 4, 1024, 128
NT = L // P
HA, DA = 16, 8
HB, DB = 16, 64
NNULL = 2
FF, NE = 512, 8
FB = FF // P
EPS = 1e-5

A_QK = 6 * DA
A_M = A_QK
A_POS = A_M + 3
A_KPOS = A_POS + 3 * NT
A_ROWS = A_KPOS + 3 * NT
A_SPLIT_Q = [0, 0, 0, 1, 1, 2]
A_SPLIT_K = [0, 1, 2, 0, 1, 0]


PROJECT_SEMS = ("x_loaded w_loaded scaled ones var_ready std_ready xn_ready xn_turned xnT_copied qk_ready v_ready "
                "part1 rest_ready part2 part3 v_copied step stored0 stored1").split()


def project_a(nc, t, d):
    with ExitStack() as c:
        def sb(n, s, dt): return c.enter_context(nc.sbuf_tensor("pa_" + n, s, dt))
        def ps(n, s, dt): return c.enter_context(nc.psum_tensor("pa_" + n, s, dt))

        x = sb("x", [P, B, NT, D], F32)
        wqkv = sb("w", [P, 3 * D], F32)
        stats, mv = sb("stats", [P, NT, 6], F32), sb("mv", [P, NT, 2], F32)
        var, std, rstd = (sb(n, [P, NT], F32) for n in ("var", "std", "rstd"))
        xn = sb("xn", [P, NT, D], F32)
        xnT = sb("xnT", [P, L], F32)
        rest = sb("rest", [P, 2, 2, L], F32)
        parts = sb("parts", [P, 2, 2, 3, L], BF16)
        psT = ps("psT", [P, L], F32)
        psQK = [ps(f"ps{n}", [P, L], F32) for n in "qk"]
        psV = ps("psV", [P, L], F32)
        s = t["sems_p"]
        block = c.enter_context(nc.Block())

        @block.sync
        def _(sp):
            for b in range(B):
                sp.dma_start(x[:, b], d["x_sorted"][b].rearrange("(t p) e -> p t e", p=P)).then_inc(s["x_loaded"], 16)
                if b == 0:
                    sp.wait_ge(s["x_loaded"], 16)
                    sp.dma_start(t["identf"][:], d["identf"]).then_inc(s["w_loaded"], 16)
                    sp.dma_start(wqkv[:], d["w_qkv"]).then_inc(s["w_loaded"], 16)
            for b in range(B):
                for i in range(2):
                    sp.wait_ge(s["part3"], 2 * b + i + 1)
                    sp.dma_start(d["parts"][b * 2 + i].rearrange("s p q -> p s q"), parts[:, b % 2, i])\
                      .then_inc(s[f"stored{b % 2}"], 16)
            for i in range(2):
                sp.wait_ge(s[f"stored{i}"], 16 * B)

        @block.vector
        def _(dve):
            v = nc.vector
            st = Steps(s["step"], 0)

            def run(ins):
                dve.wait_ge(s["step"], st.after(ins))

            def normalize(b):
                if b < 2:
                    dve.wait_ge(s["x_loaded"], 16 if b == 0 else 16 * B)
                for i in range(NT):
                    ins = v.bn_stats(stats[:, i, :], x[:, b, i, :])
                run(ins)
                for i in range(NT):
                    ins = v.bn_aggr(mv[:, i, :], stats[:, i, :])
                run(ins)
                v.tensor_scalar(var[:], mv[:, :, 1], EPS, None, ALU.add).then_inc(s["var_ready"], 1)
                dve.wait_ge(s["std_ready"], b + 1)
                run(v.reciprocal(rstd[:], std[:]))
                if b:
                    dve.wait_ge(s["xn_turned"], b)
                for i in range(NT):
                    ins = v.tensor_scalar(xn[:, i, :], x[:, b, i, :], mv[:, i, 0:1], rstd[:, i:i + 1],
                                          ALU.subtract, ALU.mult)
                ins.then_inc(s["xn_ready"], 1)
                dve.wait_ge(s["xn_ready"], b + 1)

            normalize(0)
            dve.wait_ge(s["w_loaded"], 32)
            v.tensor_scalar(wqkv[:, 0:D], wqkv[:, 0:D], float(DA) ** -0.5, None, ALU.mult).then_inc(s["scaled"], 1)
            for b in range(B):
                if b + 1 < B:
                    normalize(b + 1)
                for i in range(2):
                    dve.wait_ge(s["part1"], 2 * b + i + 1)
                    if b >= 2:
                        dve.wait_ge(s["part3"], 2 * b + i - 3)
                    v.tensor_tensor(rest[:, b % 2, i], psQK[i][:], parts[:, b % 2, i, 0], ALU.subtract)\
                     .then_inc(s["rest_ready"], 1)

        @block.gpsimd
        def _(pool):
            nc.gpsimd.memset(t["v_a"][:, :, :, DA:DA + 1], 1.0)
            for b in range(B):
                for i in range(2):
                    pool.wait_ge(s["part2"], 2 * b + i + 1)
                    nc.gpsimd.tensor_tensor(parts[:, b % 2, i, 2], rest[:, b % 2, i], parts[:, b % 2, i, 1],
                                            ALU.subtract).then_inc(s["part3"], 1)

        @block.scalar
        def _(act):
            a = nc.scalar

            def root(b):
                act.wait_ge(s["var_ready"], b + 1)
                a.activation(std[:], var[:], ACT.Sqrt).then_inc(s["std_ready"], 1)

            def copy_xn(b):
                act.wait_ge(s["xn_turned"], b + 1)
                if b:
                    act.wait_ge(s["v_ready"], b)
                a.activation(xnT[:], psT[:], ACT.Copy).then_inc(s["xnT_copied"], 1)

            root(0)
            copy_xn(0)
            for b in range(B):
                if b + 1 < B:
                    root(b + 1)
                for i in range(2):
                    act.wait_ge(s["qk_ready"], 2 * b + i + 1)
                    if b >= 2 and i == 0:
                        act.wait_ge(s[f"stored{b % 2}"], 32 * (b // 2))
                    a.activation(parts[:, b % 2, i, 0], psQK[i][:], ACT.Copy).then_inc(s["part1"], 1)
                act.wait_ge(s["v_ready"], b + 1)
                a.activation(t["v_a"][:, :, b * HA:(b + 1) * HA, 0:DA],
                             psV[:].rearrange("p (t h e) -> p t h e", t=NT, e=DA), ACT.Copy).then_inc(s["v_copied"], 1)
                if b + 1 < B:
                    copy_xn(b + 1)
                for i in range(2):
                    act.wait_ge(s["rest_ready"], 2 * b + i + 1)
                    a.activation(parts[:, b % 2, i, 1], rest[:, b % 2, i], ACT.Copy).then_inc(s["part2"], 1)

        @block.tensor
        def _(pe):
            m = nc.tensor

            def turn_xn(b):
                pe.wait_ge(s["xn_ready"], b + 1)
                if b:
                    pe.wait_ge(s["xnT_copied"], b)
                for i in range(NT):
                    ins = m.transpose(psT[:, i * P:(i + 1) * P], xn[:, i, :], t["identf"][:])
                ins.then_inc(s["xn_turned"], 1)

            pe.wait_ge(s["w_loaded"], 32)
            turn_xn(0)
            pe.wait_ge(s["scaled"], 1)
            for b in range(B):
                pe.wait_ge(s["xnT_copied"], b + 1)
                for i in range(2):
                    if b:
                        pe.wait_ge(s["rest_ready"], 2 * b + i - 1)
                    for j in range(2):
                        ins = m.matmul(psQK[i][:, j * 512:j * 512 + 512], wqkv[:, i * D:i * D + D],
                                       xnT[:, j * 512:j * 512 + 512], start=True, stop=True)
                    ins.then_inc(s["qk_ready"], 1)
                if b:
                    pe.wait_ge(s["v_copied"], b)
                for i in range(NT):
                    ins = m.matmul(psV[:, i * P:(i + 1) * P], xnT[:, i * P:(i + 1) * P], wqkv[:, 2 * D:3 * D],
                                   start=True, stop=True)
                ins.then_inc(s["v_ready"], 1)
                if b + 1 < B:
                    turn_xn(b + 1)


class Steps:

    def __init__(self, sem, base):
        self.sem, self.base, self.n = sem, base, 0

    def after(self, ins):
        ins.then_inc(self.sem, 1)
        self.n += 1
        return self.base + self.n


FFN_LOADS = {"gate": ("gw1", "gb1", "gw2", "gb2row", "gb2col", "tb2", "b2", "ones"),
             "up": ("w1", "tb1", "b1", "tw1"), "down": ("w2", "tw2")}


def ffn_tiles(nc, c, name, project):
    def sb(n, s, dt): return c.enter_context(nc.sbuf_tensor(f"{name}_{n}", s, dt))
    t = {"tw1": sb("tw1", [P, NE, FF], F32), "tw2": sb("tw2", [P, NE, FF], F32),
         "w1": sb("w1", [P, FF], F32), "w2": sb("w2", [P, FF], F32), "gw1": sb("gw1", [P, D], F32),
         "gb1": sb("gb1", [P, 1], F32), "gw2": sb("gw2", [P, NE], F32), "gb2row": sb("gb2row", [P, NE], F32),
         "gb2col": sb("gb2col", [NE, 1], F32), "b1": sb("b1", [P, FB], F32), "tb1": sb("tb1", [P, FB, NE], F32),
         "tb2": sb("tb2", [NE, D], F32), "b2": sb("b2", [1, D], F32), "ones": sb("ones", [1, P], F32)}
    if project:
        t.update({"wproj": sb("wproj", [P, D], F32), "bproj": sb("bproj", [P, D], F32),
                  "perm": sb("perm", [P, NT, L], BF16)})
    return t


FFN_SEMS = (
    "opart oT_turned oT_copied projected x_in var_ready std_ready xn_ready xn_turned xnT_copied gated relu "
    "hwide g_summed gcol_summed g_ready gcol_ready mb2_summed mw1_ready mb1_ready mw2_ready mb2_ready "
    "up gelu down x_done step stored also_loaded proj_loaded x_loaded gate_loaded up_loaded down_loaded").split()


def ffn(nc, t, d, to, also, name, project):
    with ExitStack() as c:
        def sb(n, s, dt): return c.enter_context(nc.sbuf_tensor(f"{name}_{n}", s, dt))
        def ps(n, s, dt): return c.enter_context(nc.psum_tensor(f"{name}_{n}", s, dt))

        opart = sb("opart", [P, 3, NT, P], BF16) if project else None
        orest = sb("orest", [P, NT, P], F32) if project else None
        oT = sb("oT", [P, L], F32) if project else None
        stats, mv = sb("stats", [P, NT, 6], F32), sb("mv", [P, NT, 2], F32)
        var, std, rstd = (sb(n, [P, NT], F32) for n in ("var", "std", "rstd"))
        xn = sb("xn", [P, NT, D], F32)
        xnT = [sb(f"xnT{i}", [P, L], F32) for i in range(2)]
        hrelu = sb("hrelu", [P, 512], F32)
        hsum = sb("hsum", [P, 2], F32)
        hmean = sb("hmean", [P, 1], F32)
        hwide = sb("hwide", [P, P], F32)
        g = sb("g", [P, NE], F32)
        gcol = sb("gcol", [NE, P], F32)
        mw1 = [sb(f"mw1{i}", [P, FF], F32) for i in range(2)]
        mw2 = [sb(f"mw2{i}", [P, FF], F32) for i in range(2)]
        gb = sb("gb", [P, FB, NE], F32)
        mb1 = [sb(f"mb1{i}", [P, FB], F32) for i in range(2)]
        mb2 = [sb(f"mb2{i}", [P, D], F32) for i in range(2)]
        u = sb("u", [P, 2, FB, 512], F32)
        psT = ps("psT", [P, L], F32)
        psG = ps("psG", [P, L], F32)
        psU = [ps(f"psU{i}", [P, 512], F32) for i in range(2)]
        psD = [ps(f"psD{i}", [P, 512], F32) for i in range(2)]
        s = t["sems_f"]

        def loaded(engine, what):
            count = {"proj": 2, "x": 1 + B}.get(what) or len(FFN_LOADS[what])
            if project or what not in ("proj", "x"):
                engine.wait_ge(s[what + "_loaded"], 16 * count)

        with nc.Block() as block:
            @block.vector
            def _(dve):
                v = nc.vector
                st = Steps(s["step"], 0)

                def run(ins):
                    dve.wait_ge(s["step"], st.after(ins))

                def x_of(b):
                    return t["x"][:, b, :, :]

                def split_out(b):
                    o = t["o_a"][:, :, b * HA:(b + 1) * HA, :].rearrange("p t h e -> p t (h e)")
                    if b:
                        dve.wait_ge(s["oT_turned"], b)
                    run(v.tensor_copy(opart[:, 0, :, :], o))
                    run(v.tensor_tensor(orest[:], o, opart[:, 0, :, :], ALU.subtract))
                    run(v.tensor_copy(opart[:, 1, :, :], orest[:]))
                    v.tensor_tensor(opart[:, 2, :, :], orest[:], opart[:, 1, :, :], ALU.subtract).then_inc(s["opart"], 1)
                    loaded(dve, "x")
                    run(v.tensor_tensor(x_of(b), x_of(b), t["bproj"][:].unsqueeze(1).broadcast_to([P, NT, D]), ALU.add))

                def normalize(b):
                    if project:
                        dve.wait_ge(s["projected"], b + 1)
                        v.tensor_tensor(x_of(b), x_of(b), psG[:].rearrange("p (t e) -> p t e", e=D), ALU.add)\
                         .then_inc(s["x_in"], 1)
                        dve.wait_ge(s["x_in"], b + 1)
                    for i in range(NT):
                        ins = v.bn_stats(stats[:, i, :], t["x"][:, b, i, :])
                    run(ins)
                    for i in range(NT):
                        ins = v.bn_aggr(mv[:, i, :], stats[:, i, :])
                    run(ins)
                    v.tensor_scalar(var[:], mv[:, :, 1], EPS, None, ALU.add).then_inc(s["var_ready"], 1)
                    dve.wait_ge(s["std_ready"], b + 1)
                    run(v.reciprocal(rstd[:], std[:]))
                    if b:
                        dve.wait_ge(s["xn_turned"], b)
                    for i in range(NT):
                        ins = v.tensor_scalar(xn[:, i, :], t["x"][:, b, i, :], mv[:, i, 0:1], rstd[:, i:i + 1],
                                              ALU.subtract, ALU.mult)
                    ins.then_inc(s["xn_ready"], 1)
                    dve.wait_ge(s["xn_ready"], b + 1)

                def gate(b):
                    dve.wait_ge(s["relu"], 2 * b + 2)
                    run(v.tensor_tensor(hmean[:], hsum[:, 0:1], hsum[:, 1:2], ALU.add))
                    v.tensor_scalar(hwide[:], hmean[:].broadcast_to([P, P]), 1.0 / L, None, ALU.mult)\
                     .then_inc(s["hwide"], 1)
                    dve.wait_ge(s["g_summed"], b + 1)
                    v.tensor_tensor(g[:], psG[:, 0:NE], t["gb2row"][:], ALU.add).then_inc(s["g_ready"], 1)
                    dve.wait_ge(s["g_ready"], b + 1)

                def mix(dst, src, base, ready):
                    for e in range(NE):
                        ins = v.scalar_tensor_tensor(out=dst[:], in0=src[:, e, :], scalar=g[:, e:e + 1],
                                                     in1=(base if e == 0 else dst)[:], op0=ALU.mult, op1=ALU.add)
                        if e < NE - 1:
                            run(ins)
                    ins.then_inc(ready, 1)

                def weights_up(b):
                    if b >= 2:
                        dve.wait_ge(s["down"], 2 * b - 2)
                    mix(mw1[b % 2], t["tw1"], t["w1"], s["mw1_ready"])
                    dve.wait_ge(s["mb2_summed"], b + 1)
                    v.tensor_copy(mb2[b % 2][:], psG[:, 0:D]).then_inc(s["mb2_ready"], 1)
                    run(v.tensor_tensor(gb[:], t["tb1"][:], g[:].unsqueeze(1).broadcast_to([P, FB, NE]), ALU.mult))
                    run(v.tensor_reduce(mb1[b % 2][:], gb[:], AX.X, ALU.add))
                    v.tensor_tensor(mb1[b % 2][:], mb1[b % 2][:], t["b1"][:], ALU.add).then_inc(s["mb1_ready"], 1)

                def weights_down(b):
                    mix(mw2[b % 2], t["tw2"], t["w2"], s["mw2_ready"])
                    dve.wait_ge(s["mb2_ready"], b + 1)
                    run(v.tensor_tensor(x_of(b), x_of(b), mb2[b % 2][:].unsqueeze(1).broadcast_to([P, NT, D]), ALU.add))

                def add_down(b, j):
                    xh = t["x"][:, b, j * 4:j * 4 + 4, :]
                    dve.wait_ge(s["down"], 2 * b + j + 1)
                    v.tensor_tensor(xh, xh, psD[j][:].rearrange("p (t e) -> p t e", e=D), ALU.add).then_inc(s["x_done"], 1)

                def ready(b):
                    gate(b)
                    if project and b + 1 < B:
                        split_out(b + 1)
                    if b == 0:
                        loaded(dve, "up")
                    weights_up(b)
                    if b == 0:
                        loaded(dve, "down")
                    if project:
                        weights_down(b)
                    if b + 1 < B:
                        normalize(b + 1)
                    if not project:
                        weights_down(b)

                if project:
                    split_out(0)
                normalize(0)
                loaded(dve, "gate")
                ready(0)
                for b in range(B):
                    if b + 1 < B:
                        ready(b + 1)
                    add_down(b, 0)
                    add_down(b, 1)

            @block.scalar
            def _(act):
                a = nc.scalar

                def copy_out(b):
                    act.wait_ge(s["oT_turned"], b + 1)
                    if b:
                        act.wait_ge(s["projected"], b)
                    a.activation(oT[:], psT[:], ACT.Copy).then_inc(s["oT_copied"], 1)

                def root(b):
                    act.wait_ge(s["var_ready"], b + 1)
                    a.activation(std[:], var[:], ACT.Sqrt).then_inc(s["std_ready"], 1)

                def copy_xn(b):
                    act.wait_ge(s["xn_turned"], b + 1)
                    if b >= 2:
                        act.wait_ge(s["up"], 8 * b - 8)
                    a.activation(xnT[b % 2][:], psT[:], ACT.Copy).then_inc(s["xnT_copied"], 1)

                def gate(b):
                    for j in range(2):
                        act.wait_ge(s["gated"], 2 * b + j + 1)
                        if b or j:
                            act.wait_ge(s["relu"], 2 * b + j)
                        if b and j == 0:
                            act.wait_ge(s["hwide"], b)
                        a.activation(hrelu[:], psG[:, j * 512:j * 512 + 512], ACT.Relu, bias=t["gb1"][:, 0:1],
                                     accum_out=hsum[:, j:j + 1]).then_inc(s["relu"], 1)

                def gates(b):
                    act.wait_ge(s["gcol_summed"], b + 1)
                    a.activation(gcol[:], psG[0:NE, 512:512 + P], ACT.Identity, bias=t["gb2col"][:, 0:1])\
                     .then_inc(s["gcol_ready"], 1)

                def gelu(b, j):
                    if j == 0:
                        act.wait_ge(s["mb1_ready"], b + 1)
                    if b:
                        act.wait_ge(s["down"], 2 * b - 1 + j)
                    for f in range(FB):
                        act.wait_ge(s["up"], 8 * b + 4 * j + f + 1)
                        a.activation(u[:, j, f, :], psU[f % 2][:], ACT.Gelu_apprx_tanh, bias=mb1[b % 2][:, f:f + 1])\
                         .then_inc(s["gelu"], 1)

                def prepare(b):
                    if b < B:
                        if project:
                            copy_out(b)
                        root(b)

                prepare(0)
                copy_xn(0)
                loaded(act, "gate")
                gate(0)
                gates(0)
                prepare(1)
                for b in range(B):
                    gelu(b, 0)
                    if b + 1 < B:
                        copy_xn(b + 1)
                        gate(b + 1)
                    gelu(b, 1)
                    if b + 1 < B:
                        gates(b + 1)
                    prepare(b + 2)

            @block.tensor
            def _(pe):
                m = nc.tensor

                def turn_out(b):
                    pe.wait_ge(s["opart"], b + 1)
                    if b:
                        pe.wait_ge(s["xnT_copied"], b)
                    for j in range(2):
                        for i in range(NT):
                            for k in range(3):
                                ins = m.matmul(psT[:, j * 512:j * 512 + 512], opart[:, k, i, :],
                                               t["perm"][:, i, j * 512:j * 512 + 512],
                                               start=(i == k == 0), stop=(i == NT - 1 and k == 2))
                    ins.then_inc(s["oT_turned"], 1)

                def project_out(b):
                    pe.wait_ge(s["oT_copied"], b + 1)
                    if b:
                        pe.wait_ge(s["mb2_ready"], b)
                    for i in range(NT):
                        ins = m.matmul(psG[:, i * P:(i + 1) * P], oT[:, i * P:(i + 1) * P], t["wproj"][:],
                                       start=True, stop=True)
                    ins.then_inc(s["projected"], 1)

                def turn_xn(b):
                    pe.wait_ge(s["xn_ready"], b + 1)
                    if project:
                        pe.wait_ge(s["oT_copied"], b + 1)
                    elif b:
                        pe.wait_ge(s["xnT_copied"], b)
                    for i in range(NT):
                        ins = m.transpose(psT[:, i * P:(i + 1) * P], xn[:, i, :], t["identf"][:])
                    ins.then_inc(s["xn_turned"], 1)

                def gate(b):
                    pe.wait_ge(s["xnT_copied"], b + 1)
                    if project:
                        pe.wait_ge(s["x_in"], b + 1)
                    if b:
                        pe.wait_ge(s["mb2_ready"], b)
                        pe.wait_ge(s["gcol_ready"], b)
                    for j in range(2):
                        m.matmul(psG[:, j * 512:j * 512 + 512], t["gw1"][:], xnT[b % 2][:, j * 512:j * 512 + 512],
                                 start=True, stop=True).then_inc(s["gated"], 1)

                def gates(b):
                    pe.wait_ge(s["relu"], 2 * b + 2)
                    pe.wait_ge(s["hwide"], b + 1)
                    m.matmul(psG[:, 0:NE], hwide[:], t["gw2"][:], start=True, stop=True).then_inc(s["g_summed"], 1)
                    m.matmul(psG[0:NE, 512:512 + P], t["gw2"][:], hwide[:], start=True, stop=True)\
                     .then_inc(s["gcol_summed"], 1)
                    pe.wait_ge(s["gcol_ready"], b + 1)
                    pe.wait_ge(s["g_ready"], b + 1)
                    m.matmul(psG[:, 0:D], gcol[:], t["tb2"][:], start=True, stop=False)
                    m.matmul(psG[:, 0:D], t["ones"][0:1, :], t["b2"][:], start=False, stop=True)\
                     .then_inc(s["mb2_summed"], 1)

                def up(b, j):
                    if j == 0:
                        pe.wait_ge(s["mw1_ready"], b + 1)
                    for f in range(FB):
                        n = 8 * b + 4 * j + f
                        if n >= 2:
                            pe.wait_ge(s["gelu"], n - 1)
                        m.matmul(psU[f % 2][:], mw1[b % 2][:, f * P:(f + 1) * P], xnT[b % 2][:, j * 512:j * 512 + 512],
                                 start=True, stop=True).then_inc(s["up"], 1)

                def down(b, j):
                    pe.wait_ge(s["gelu"], 8 * b + 4 * j + 4)
                    if j == 0:
                        pe.wait_ge(s["mw2_ready"], b + 1)
                    if b:
                        pe.wait_ge(s["x_done"], 2 * b - 1 + j)
                    for i in range(4):
                        for f in range(FB):
                            ins = m.matmul(psD[j][:, i * P:(i + 1) * P], u[:, j, f, i * P:(i + 1) * P],
                                           mw2[b % 2][:, f * P:(f + 1) * P], start=(f == 0), stop=(f == FB - 1))
                    ins.then_inc(s["down"], 1)

                def prepare(b):
                    if project and b < B:
                        turn_out(b)
                        project_out(b)

                loaded(pe, "proj")
                prepare(0)
                turn_xn(0)
                loaded(pe, "gate")
                gate(0)
                gates(0)
                prepare(1)
                for b in range(B):
                    up(b, 0)
                    if b + 1 < B:
                        turn_xn(b + 1)
                        gate(b + 1)
                    up(b, 1)
                    if b + 1 < B:
                        gates(b + 1)
                    if project and b + 2 < B:
                        turn_out(b + 2)
                    down(b, 0)
                    if project and b + 2 < B:
                        project_out(b + 2)
                    down(b, 1)

            @block.sync
            def _(sp):
                if project:
                    for n in ("perm", "wproj"):
                        sp.dma_start(t[n][:], d[n]).then_inc(s["proj_loaded"], 16)
                    sp.dma_start(t["bproj"][:], d["bproj"].broadcast_to([P, D])).then_inc(s["x_loaded"], 16)
                    for b in range(B):
                        sp.dma_start(t["x"][:, b], d["x"][b].rearrange("(t p) e -> p t e", p=P)).then_inc(s["x_loaded"], 16)
                for what, names in FFN_LOADS.items():
                    for n in names:
                        of = d[n].broadcast_to([P, NE]) if n == "gb2row" else d[n]
                        sp.dma_start(t[n][:], of).then_inc(s[what + "_loaded"], 16)
                for n in also:
                    sp.dma_start(t[n][:], d[n]).then_inc(s["also_loaded"], 16)
                if also:
                    sp.wait_ge(s["also_loaded"], 16 * len(also))
                if to is not None:
                    for b in range(B):
                        sp.wait_ge(s["x_done"], 2 * b + 2)
                        sp.dma_start(to[b].rearrange("(t p) e -> p t e", p=P), t["x"][:, b]).then_inc(s["stored"], 16)
                    sp.wait_ge(s["stored"], 16 * B)


def attend_a(nc, t, d, g):
    NPAIR = HA
    FIRST = 4
    NLOAD = 12 * 16
    NCONST = 4
    AHEAD = 6
    LAST = NT - 1 - AHEAD // 2
    TURN = LAST + 2
    VW = 32

    def events(i):
        out = []
        for kb in range(NT):
            ahead = 1 if kb <= LAST else 2
            if i + ahead < NPAIR:
                out += [(kb, "max", j) for j in range(2)]
            if kb == 3 and i > 0:
                out.append((kb, "out", 0))
            if kb == TURN and i + 1 < NPAIR:
                out.append((kb, "turn", 0))
        return out

    first = 2 * NT + 1 + AHEAD
    start = {0: first}
    for n in range(NPAIR):
        start[n + 1] = start[n] + len(events(n))

    def use(i, kb, kind, tile=0):
        r = start[i] + events(i).index((kb, kind, tile))
        return r, r % 2

    def use_of_turn(p):
        return (2 * NT, 0) if p == 0 else use(p - 1, TURN, "turn")

    with ExitStack() as c:
        def sb(n, s, dt): return c.enter_context(nc.sbuf_tensor(n, s, dt))
        def ps(n, s, dt): return c.enter_context(nc.psum_tensor(n, s, dt))

        q = sb("aa_q", [A_ROWS, 2 * HA, L], BF16)
        k = sb("aa_k", [A_ROWS, 2 * HA, L], BF16)
        near = sb("aa_near", [P, NT, P], F32)
        prob = sb("aa_prob", [P, 4, 2, L], F32)
        vst = sb("aa_vst", [P, 2, NT, 2, VW], F32)
        mx = sb("aa_mx", [P, 2 * NT], F32)
        mrest = sb("aa_mrest", [P, 2 * NT], F32)
        mparts = sb("aa_mparts", [P, P // (2 * NT), 2 * NT], BF16)
        mT = sb("aa_mT", [3 * 2 * NT, P], BF16)
        oT = sb("aa_oT", [P, 512], F32)
        rsum = sb("aa_rsum", [P, NT // 2, 4], F32)
        warm = sb("aa_warm", [P, 1], F32)
        psS = [ps(f"aa_psS{i}", [P, 512], F32) for i in range(3)]
        psM = [ps(f"aa_psM{i}", [P, L], F32) for i in range(2)]
        psO = ps("aa_psO", [P, 512], F32)
        (consts, loaded, s_ready, exp_done, near_done, pv_done, use_ready, use_done, m_split, m_loaded,
         v_zeroed, m_zeroed, v_staged, oT_ready, inverted) = (t["sems_a"][n] for n in A_SEMS)
        block = c.enter_context(nc.Block())

        @block.sync
        def _(sp):
            def load(b, first, last):
                for i in range(6):
                    for side, to, of in ((0, q, A_SPLIT_Q[i]), (1, k, A_SPLIT_K[i])):
                        src = d["parts"][ds(g * 4 + b * 2 + side, 1), of, first * DA:last * DA, :]
                        sp.dma_start(to[i * DA:(i + 1) * DA, b * HA + first:b * HA + last, :],
                                     src.rearrange("o (h e) q -> e (o h) q", e=DA)).then_inc(loaded, 16)

            load(0, 0, FIRST)
            sp.wait_ge(loaded, NLOAD)
            sp.dma_start(k[A_M:A_ROWS], d["a_krows"].unsqueeze(1).broadcast_to([A_ROWS - A_M, 2 * HA, L]))\
              .then_inc(consts, 16)
            sp.dma_start(q[A_POS:A_ROWS], d["a_qrows"].unsqueeze(1).broadcast_to([A_ROWS - A_POS, 2 * HA, L]))\
              .then_inc(consts, 16)
            sp.dma_start(near[:], d["near"]).then_inc(consts, 16)
            sp.dma_start(t["identb"][:], d["identb"]).then_inc(consts, 16)
            load(0, FIRST, HA)
            for p in range(NPAIR):
                if p == 1:
                    sp.wait_ge(loaded, 2 * NLOAD)
                    load(1, 0, HA)
                sp.wait_ge(use_done, use_of_turn(p)[0] + 1)
                to = q[A_M:A_M + 3, p * 2:p * 2 + 2, :].rearrange("r h (i e) -> r (h i) e", e=P)
                sp.dma_start(to, mT[0:6 * NT, :]).then_inc(m_loaded, 16)
                sp.wait_ge(m_loaded, 16 * p + 16)
            sp.wait_ge(loaded, 3 * NLOAD)

        @block.gpsimd
        def _(pool):
            nc.gpsimd.memset(vst[:], 0.0).then_inc(v_zeroed, 1)
            pool.wait_ge(v_zeroed, 1)

            def stage(i, odd):
                if i >= 2:
                    pool.wait_ge(pv_done, i * NT - NT)
                nc.gpsimd.tensor_copy(vst[:, odd, :, :, 0:DA + 1], t["v_a"][:, :, ds(g * 2 * HA + i * 2, 2), :])\
                  .then_inc(v_staged, 1)

            def pair(i, odd):
                for kb in range(NT):
                    pool.wait_ge(exp_done, (i * NT + kb) * 4 + 3 + kb // (NT // 2))
                    p = prob[:, kb % 4, :, kb * P:(kb + 1) * P]
                    nc.gpsimd.tensor_tensor(p, p, near[:, kb, :].unsqueeze(1).broadcast_to([P, 2, P]), ALU.mult)\
                      .then_inc(near_done, 1)
                    if kb == 3 and i < NPAIR - 1:
                        stage(i + 1, 1 - odd)

            stage(0, 0)
            pool.wait_ge(consts, 16 * NCONST)
            for i in range(NPAIR):
                pair(i, i % 2)

        @block.scalar
        def _(act):
            nc.scalar.activation(warm[:], t["identf"][:, 0:1], ACT.Exp)

            def take_out(i, odd):
                act.wait_ge(pv_done, i * NT + NT)
                if i > 0:
                    act.wait_ge(use_ready, use(i, 3, "out")[0] + 1)
                nc.scalar.activation(oT[:], psO[:], ACT.Copy).then_inc(oT_ready, 1)

            def pair(i, odd):
                for kb in range(NT):
                    at = i * NT + kb
                    for h in range(2):
                        for half in range(2):
                            act.wait_ge(s_ready, at * 4 + 2 * h + half + 1)
                            if h == half == 0 and at >= 4:
                                act.wait_ge(pv_done, at - 3)
                            nc.scalar.activation(prob[:, kb % 4, h, half * 512:half * 512 + 512],
                                                 psS[(at * 4 + 2 * h + half) % 3][:],
                                                 ACT.Exp).then_inc(exp_done, 1)
                    if kb == 1 and i > 0:
                        take_out(i - 1, 1 - odd)

            for i in range(NPAIR):
                pair(i, i % 2)
            take_out(NPAIR - 1, 1)

        @block.vector
        def _(dve):
            v = nc.vector

            def maximum(p, tile, r, which):
                dve.wait_ge(use_ready, r + 1)
                if tile == 0 and p > 0:
                    dve.wait_ge(m_split, 4 * p)
                v.tensor_reduce(mx[:, tile:tile + 1], psM[which][:], AX.X, ALU.max,
                                negate=True).then_inc(use_done, 1)

            def split(p, r):
                dve.wait_ge(use_done, r + 1)
                v.tensor_copy(mparts[:, 0, :], mx[:]).then_inc(m_split, 1)
                dve.wait_ge(m_split, 4 * p + 1)
                v.tensor_tensor(mrest[:], mx[:], mparts[:, 0, :], ALU.subtract).then_inc(m_split, 1)
                dve.wait_ge(m_split, 4 * p + 2)
                v.tensor_copy(mparts[:, 1, :], mrest[:]).then_inc(m_split, 1)
                dve.wait_ge(m_split, 4 * p + 3)
                v.tensor_tensor(mparts[:, 2, :], mrest[:], mparts[:, 1, :], ALU.subtract).then_inc(m_split, 1)

            def take_turned(p):
                r, which = use_of_turn(p)
                dve.wait_ge(use_ready, r + 1)
                if p > 0:
                    dve.wait_ge(m_loaded, 16 * p)
                v.tensor_copy(mT[:], psM[which][0:3 * 2 * NT, 0:P // 2].bitcast(BF16)).then_inc(use_done, 1)

            def normalize(i, r, which):
                o = psM[which][:, 0:4 * P].rearrange("p (c g e) -> p c g e", c=NT // 2, e=VW)
                dve.wait_ge(use_ready, r + 1)
                v.reciprocal(rsum[:], o[:, :, :, DA]).then_inc(inverted, 1)
                dve.wait_ge(inverted, 2 * i + 1)
                for h in range(2):
                    to = t["o_a"][:, :, ds(g * 2 * HA + i * 2 + h, 1), :].rearrange("p (f c) o e -> p f c (o e)", f=2)
                    s = v.tensor_tensor(to, o[:, :, 2 * h:2 * h + 2, 0:DA].rearrange("p c f e -> p f c e"),
                                        rsum[:, :, 2 * h:2 * h + 2].rearrange("p c f -> p f c").unsqueeze(3)
                                        .broadcast_to([P, 2, NT // 2, DA]), ALU.mult)
                    s.then_inc(use_done if h else inverted, 1)
                dve.wait_ge(use_done, r + 1)

            def pair(i, odd):
                for kb, kind, tile in events(i):
                    r, which = use(i, kb, kind, tile)
                    if kind == "max" and kb <= LAST:
                        maximum(i + 1, AHEAD + 2 * kb + tile, r, which)
                        if kb == LAST and tile == 1:
                            split(i + 1, r)
                    elif kind == "max":
                        maximum(i + 2, 2 * (kb - LAST - 1) + tile, r, which)
                    elif kind == "turn":
                        take_turned(i + 1)
                    else:
                        normalize(i - 1, r, which)

            v.memset(mparts[:], 0.0).then_inc(m_zeroed, 1)
            dve.wait_ge(m_zeroed, 1)
            for r in range(2 * NT):
                maximum(0, r, r, r % 2)
            split(0, 2 * NT - 1)
            take_turned(0)
            for n in range(AHEAD):
                maximum(1, n, 2 * NT + 1 + n, (2 * NT + 1 + n) % 2)
            for i in range(NPAIR):
                pair(i, i % 2)
            normalize(NPAIR - 1, start[NPAIR], start[NPAIR] % 2)

        @block.tensor
        def _(pe):
            mm = nc.tensor

            def head(x, rows, n, a, b_):
                return x[0:rows, n, a:b_]

            def scores(i, kb):
                if i == kb == 0:
                    pe.wait_ge(consts, 16 * NCONST)
                if kb == 0:
                    pe.wait_ge(m_loaded, 16 * i + 16)
                for h in range(2):
                    for half in range(2):
                        at = (i * NT + kb) * 4 + 2 * h + half
                        if at >= 3:
                            pe.wait_ge(exp_done, at - 2)
                        mm.matmul(psS[at % 3][:], head(k, A_ROWS, i * 2 + h, kb * P, (kb + 1) * P),
                                  head(q, A_ROWS, i * 2 + h, half * 512, half * 512 + 512),
                                  start=True, stop=True).then_inc(s_ready, 1)
                        if half == 1:
                            yield

            def max_scores(p, tile, r, which):
                if tile == 0:
                    pe.wait_ge(loaded, NLOAD * (1 if 2 * p < FIRST else 2 if 2 * p < HA else 3))
                if r >= 2:
                    pe.wait_ge(use_done, r - 1)
                n, qb = p * 2 + tile // NT, tile % NT
                for half in range(2):
                    s = mm.matmul(psM[which][:, half * 512:half * 512 + 512], head(q, A_QK, n, qb * P, (qb + 1) * P),
                                  head(k, A_QK, n, half * 512, half * 512 + 512), start=True, stop=True)
                s.then_inc(use_ready, 1)

            def turn_max(p):
                r, which = use_of_turn(p)
                if p == 0:
                    pe.wait_ge(consts, 16 * NCONST)
                pe.wait_ge(m_split, 4 * p + 4)
                pe.wait_ge(use_done, r - 1)
                mm.transpose(psM[which][:, 0:P // 2].bitcast(BF16),
                             mparts[:].rearrange("p s t -> p (s t)"), t["identb"][:]).then_inc(use_ready, 1)

            def turn_out(i, r, which):
                pe.wait_ge(oT_ready, i + 1)
                pe.wait_ge(use_done, r - 1)
                for qc in range(NT // 2):
                    s = mm.transpose(psM[which][:, qc * P:(qc + 1) * P], oT[:, qc * P:(qc + 1) * P], t["identf"][:])
                s.then_inc(use_ready, 1)

            def values(i, kb, odd):
                at = i * NT + kb
                pe.wait_ge(exp_done, at * 4 + 4)
                pe.wait_ge(near_done, at + 1)
                if kb == 0:
                    pe.wait_ge(v_staged, i + 1)
                    if i > 0:
                        pe.wait_ge(oT_ready, i)
                for h in range(2):
                    for half in range(2):
                        c4 = 2 * h + half
                        s = mm.matmul(psO[c4 * VW:(c4 + 1) * VW, :], vst[:, odd, kb, h, :],
                                      prob[:, kb % 4, h, half * 512:half * 512 + 512],
                                      start=(kb == 0), stop=(kb == NT - 1), skip_group_check=True)
                s.then_inc(pv_done, 1)

            def pair(i, odd):
                these = events(i)
                for kb in range(NT):
                    todo = [e for e in these if e[0] == kb]
                    steps = scores(i, kb)
                    for n in range(2):
                        next(steps)
                        for e in todo[n:] if n else todo[:1]:
                            r, which = use(i, *e)
                            if e[1] == "max" and kb <= LAST:
                                max_scores(i + 1, AHEAD + 2 * kb + e[2], r, which)
                            elif e[1] == "max":
                                max_scores(i + 2, 2 * (kb - LAST - 1) + e[2], r, which)
                            elif e[1] == "turn":
                                turn_max(i + 1)
                            else:
                                turn_out(i - 1, r, which)
                    if kb >= 2:
                        values(i, kb - 2, odd)
                    elif i > 0:
                        values(i - 1, kb + NT - 2, 1 - odd)

            for r in range(2 * NT):
                max_scores(0, r, r, r % 2)
            turn_max(0)
            for n in range(AHEAD):
                max_scores(1, n, 2 * NT + 1 + n, (2 * NT + 1 + n) % 2)
            for i in range(NPAIR):
                pair(i, i % 2)
            values(NPAIR - 1, NT - 2, 1)
            values(NPAIR - 1, NT - 1, 1)
            turn_out(NPAIR - 1, start[NPAIR], start[NPAIR] % 2)


A_SEMS = ("consts loaded s_ready exp_done near_done pv_done use_ready use_done m_split m_loaded v_zeroed "
          "m_zeroed v_staged oT_ready inverted").split()


def attention_a(nc, t, d):
    with ExitStack() as c:
        t["sems_a"] = {n: c.enter_context(nc.semaphore("aa_" + n)) for n in A_SEMS}
        with nc.Fori(0, B // 2) as g:
            attend_a(nc, t, d, g)
            restart(nc, t["sems_a"])


HALF = HB // 2
B_BIAS = 3
B_BLOCK = 3 * NT
B_M = DB + B_BIAS + B_BLOCK
B_ROWS = B_M + 3
UNITS = NT * (NT + 1) // 2 * P // 512
BLOCKS = [(q, kb) for q in range(NT) for kb in range(q + 1)]
MAX_TILES = [[(7, 0)], [(6, 0)], [(5, 0)], [(4, 0)], [(3, 0), (2, 512)], [(1, 0), (0, 256)]]
FIRST_TILES = MAX_TILES[4::-1] + MAX_TILES[5:]
USES = len(MAX_TILES) + 1
NULL_COL = 512
T_P1, T_P1B, T_P2, T_M = 0, 32, 64, 96
RING = 6
LAG = 3
LO_POOL = (0, 1, 5, 7)
ROW_LOADS = 2
B_SEMS = ("n_step n_var n_std n_xn n_turned rows rows0 rows1 rows2 rows3 proj q_sq k_sq summed rooted rn "
          "q_normed k_normed q_scaled q_hi k_hi v_hi q_lo k_lo v_lo qa_turned ka_turned kb_turned qa_done "
          "ka_done kb_done copied m_loaded use_ready use_done s_ready exp_done null_sub null_exp null_parts "
          "nm_ready nm_chain pool_chain lo_dve lo_pool pv_done o_ready o_inverted o_done turned_out out_copied "
          "out_ready out_added").split()


B_WEIGHTS = ("wq", "wk", "wv", "wout", "norm_g", "norm_b", "identh", "upper", "lower")


def weights_b(nc, c):
    def sb(n, s, dt): return c.enter_context(nc.sbuf_tensor("wb_" + n, s, dt))
    return {"wq": sb("wq", [P, HB * DB], F32), "wk": sb("wk", [P, HB * DB], F32), "wv": sb("wv", [P, HB * DB], F32),
            "wout": sb("wout", [P, HB * DB // P, D], F32), "norm_g": sb("norm_g", [P, 1], F32),
            "norm_b": sb("norm_b", [P, 1], F32), "identh": sb("identh", [P, P], F16),
            "upper": sb("upper", [P, P], BF16), "lower": sb("lower", [P, P], BF16)}


def tiles_b(nc, c):
    def sb(n, s, dt): return c.enter_context(nc.sbuf_tensor("tb_" + n, s, dt))
    return {
        "c": sb("c", [P, DB], F32),
        "null_a": sb("null_a", [P, HB, NNULL], F16), "null_b": sb("null_b", [B_M, HB, NNULL], F16),
        "null_v": sb("null_v", [T_M, HB, NT, DB + 1], F16),
        "sq": sb("sq", [P, 4, HALF * DB], F32),
        "ss": sb("ss", [P, 2, 2, HALF], F32), "root": sb("root", [P, 2, 2, HALF], F32),
        "rn": sb("rn", [P, 2, 2, HALF], F32),
        "hi": sb("hi", [P, RING, 512], F16), "lo": sb("lo", [P, RING, 512], F16),
        "full": sb("full", [P, RING, 512], F32),
        "nm": sb("nm", [P, NT], F32), "rest": sb("rest", [P, NT], F32), "nmax": sb("nmax", [P, NT], F32),
        "null": sb("null", [P, NT, NNULL], F32), "nullx": sb("nullx", [P, NT, NNULL], F32),
        "nullp": sb("nullp", [P, NT * NNULL], F32),
        "turn": sb("turn", [P, P], F16), "turned": sb("turned", [P, P], F16), "rsum": sb("rsum", [P, NT], F32),
        "warm": sb("warm", [P, 1], F32), "oT": sb("oT", [P, 2, HALF * DB], F32),
        "xlT": sb("xlT", [P, L], F32), "xqT": sb("xqT", [P, L], F32),
        "qa": sb("qa", [P, HALF, L], F16), "ka": sb("ka", [P, HALF, L], F16),
        "qb": sb("qb", [B_ROWS, HALF, L], F16), "kb": sb("kb", [B_ROWS, HALF, L], F16),
        "kc": sb("kc", [B_M, HALF, L], F16),
        "v1": sb("v1", [P, NT, HALF, DB + 1], F16), "v2": sb("v2", [P, NT, HALF, DB], F16),
        "sems_b": [{n: c.enter_context(nc.semaphore(f"b{hf}_{n}")) for n in B_SEMS} for hf in range(2)],
    }


def load_b(nc, t, d):
    with ExitStack() as c:
        small = t["oT"][:].rearrange("p a b -> p (a b)")

        def taken(first, n):
            return small[:, first:first + n]

        ks, halves, diag = taken(0, DB), taken(DB, P), taken(DB + P, NT)[0:T_M]
        first = DB + P + NT
        nk, sq, root = (taken(first + i * HB * NNULL, HB * NNULL).rearrange("p (h n) -> p h n", n=NNULL)
                        for i in range(3))
        width = HB * (DB + 1)
        nv = t["full"][:].rearrange("p a b -> p (a b)")[0:T_M, 0:width].rearrange("p (h e) -> p h e", e=DB + 1)
        nvp = t["hi"][:].rearrange("p a b -> p (a b)")[0:T_M, 0:width].rearrange("p (h e) -> p h e", e=DB + 1)
        psN = c.enter_context(nc.psum_tensor("lb_psN", [P, 512], F32))
        landed, step, rooted, summed = (c.enter_context(nc.semaphore("lb_" + n)) for n in ("landed", "step", "root", "sum"))
        n_dma = 7 + HALF
        block = c.enter_context(nc.Block())

        @block.sync
        def _(sp):
            sp.dma_start(t["c"][:], d["q_scale"].broadcast_to([P, DB])).then_inc(landed, 16)
            sp.dma_start(ks[:], d["k_scale"].broadcast_to([P, DB])).then_inc(landed, 16)
            for i in range(2):
                sp.dma_start(nk[i * DB:(i + 1) * DB], d["null_k"]).then_inc(landed, 16)
            sp.dma_start(diag[:], d["b_diag"]).then_inc(landed, 16)
            sp.dma_start(t["null_b"][DB:B_M], d["b_nrows"]).then_inc(landed, 16)
            sp.dma_start(nv[:, :, 0:DB], d["null_v"]).then_inc(landed, 16)
            for n in range(HALF):
                sp.dma_start(t["qb"][DB:B_M, n, :], d["b_qrows"]).then_inc(landed, 16)
            sp.wait_ge(landed, 16 * n_dma)

        @block.tensor
        def _(pe):
            pe.wait_ge(step, 5)
            nc.tensor.matmul(psN[:, 0:HB * NNULL], halves[:], sq[:].rearrange("p h n -> p (h n)"),
                             start=True, stop=True).then_inc(summed, 1)

        @block.scalar
        def _(act):
            act.wait_ge(summed, 1)
            nc.scalar.activation(root[:], psN[:, 0:HB * NNULL].rearrange("p (h n) -> p h n", n=NNULL), ACT.Sqrt)\
              .then_inc(rooted, 1)

        @block.vector
        def _(dve):
            v = nc.vector
            st = Steps(step, 0)

            def run(ins):
                dve.wait_ge(step, st.after(ins))

            run(v.memset(halves[:], 0.5))
            run(v.memset(t["v1"][:, :, :, DB:DB + 1], 1.0))
            run(v.memset(nv[:, :, DB:DB + 1], 1.0))
            dve.wait_ge(landed, 16 * n_dma)
            run(v.scalar_tensor_tensor(out=t["c"][:], in0=t["c"][:], scalar=8.0, in1=ks[:], op0=ALU.mult, op1=ALU.mult))
            run(v.tensor_tensor(sq[:], nk[:], nk[:], ALU.mult))
            run(v.tensor_copy(nvp[:], nv[:]))
            lo = slice(T_P1B, T_P2)
            run(v.tensor_tensor(nvp[lo], nv[lo], nvp[lo], ALU.subtract))
            for i in range(NT):
                run(v.tensor_scalar(t["null_v"][:, :, i, :], nvp[:], diag[:, i:i + 1], None, ALU.mult))
            dve.wait_ge(rooted, 1)
            run(v.tensor_scalar(root[:], root[:], 1e-12, None, ALU.max))
            run(v.reciprocal(root[:], root[:]))
            run(v.tensor_tensor(nk[:], nk[:], root[:], ALU.mult))
            run(v.tensor_copy(t["null_a"][:], nk[:]))
            run(v.tensor_tensor(t["null_b"][0:DB], nk[0:DB], t["null_a"][0:DB], ALU.subtract))


class NormB:

    def __init__(self, nc, t, b):
        self.nc, self.t, self.b, self.s = nc, t, b, t["sems_b"][1]
        self.xl, self.xq = (t["full"][:, 2 * i:2 * i + 2, :].rearrange("p a b -> p (a b)")
                            .rearrange("p (t e) -> p t e", e=D) for i in range(2))
        small = t["hi"][:].rearrange("p a b -> p (a b)").bitcast(F32)
        self.stats = small[:, 0:6 * NT].rearrange("p (t e) -> p t e", e=6)
        self.mv = small[:, 6 * NT:8 * NT].rearrange("p (t e) -> p t e", e=2)
        self.var, self.std, self.rstd = (small[:, (8 + i) * NT:(9 + i) * NT] for i in range(3))

    def normalize(self, dve, j):
        v, s = self.nc.vector, self.s

        def x(i):
            return self.xl[:, i, :] if j else self.t["x"][:, ds(self.b, 1), i, :].rearrange("p o e -> p (o e)")

        if j:
            dve.wait_ge(s["n_xn"], j)
        for i in range(NT):
            ins = v.bn_stats(self.stats[:, i, :], x(i))
        ins.then_inc(s["n_step"], 1)
        dve.wait_ge(s["n_step"], 3 * j + 1)
        for i in range(NT):
            ins = v.bn_aggr(self.mv[:, i, :], self.stats[:, i, :])
        ins.then_inc(s["n_step"], 1)
        dve.wait_ge(s["n_step"], 3 * j + 2)
        v.tensor_scalar(self.var, self.mv[:, :, 1], EPS, None, ALU.add).then_inc(s["n_var"], 1)
        dve.wait_ge(s["n_std"], j + 1)
        v.reciprocal(self.rstd, self.std).then_inc(s["n_step"], 1)
        dve.wait_ge(s["n_step"], 3 * j + 3)
        to = self.xq if j else self.xl
        for i in range(NT):
            ins = v.tensor_scalar(to[:, i, :], x(i), self.mv[:, i, 0:1], self.rstd[:, i:i + 1],
                                  ALU.subtract, ALU.mult)
        ins.then_inc(s["n_xn"], 1)

    def root(self, act, j):
        act.wait_ge(self.s["n_var"], j + 1)
        self.nc.scalar.activation(self.std, self.var, ACT.Sqrt).then_inc(self.s["n_std"], 1)

    def turn(self, pe, j, to):
        pe.wait_ge(self.s["n_xn"], j + 1)
        for i in range(NT):
            ins = self.nc.tensor.transpose(to[i // 4][:, i % 4 * P:(i % 4 + 1) * P], (self.xq if j else self.xl)[:, i, :],
                                           self.t["identf"][:])
        ins.then_inc(self.s["n_turned"], 1)

    def take(self, act, j, of):
        t = self.t
        act.wait_ge(self.s["n_turned"], j + 1)
        for i in range(2):
            cols = slice(i * 512, (i + 1) * 512)
            if j:
                self.nc.scalar.activation(t["xqT"][:, cols], of[i], ACT.Identity, bias=t["norm_b"][:, 0:1],
                                          scale=t["norm_g"][:, 0:1])
            else:
                self.nc.scalar.activation(t["xlT"][:, cols], of[i], ACT.Copy)


def norm_b(nc, t):
    to = [t[n][:, k:k + 512] for n, k in (("psM0", 0), ("psM0", 512), ("psM1", 0), ("psM1", 512))]
    norm = NormB(nc, t, 0)
    with nc.Block() as block:
        @block.vector
        def _(dve):
            for j in range(2):
                norm.normalize(dve, j)

        @block.scalar
        def _(act):
            for j in range(2):
                norm.root(act, j)
            for j in range(2):
                norm.take(act, j, to[2 * j:2 * j + 2])

        @block.tensor
        def _(pe):
            for j in range(2):
                norm.turn(pe, j, to[2 * j:2 * j + 2])


def project_tile(nc, t, pe, hf, i, j):
    s, W = t["sems_b"][hf], HALF * DB
    x, w, done = (("xqT", "wq", "q_normed"), ("xlT", "wk", "k_normed"), ("xlT", "wv", "v_lo"))[j]
    out = (t["psM0"][:, i % 2 * W:(i % 2 + 1) * W], t["psM1"][:, i % 2 * W:(i % 2 + 1) * W], t[f"psO{i % 2}"][:])[j]
    if i >= 2:
        pe.wait_ge(s[done], i - 1)
    elif hf and i == 0:
        last = t["sems_b"][0]
        if j == 0:
            pe.wait_ge(last["use_done"], HALF * USES)
        if j == 2:
            pe.wait_ge(last["o_done"], 2 * HALF)
    nc.tensor.matmul(out, t[x][:, i * P:(i + 1) * P], t[w][:, hf * W:(hf + 1) * W], start=True, stop=True)\
      .then_inc(s["proj"], 1)


def project_b(nc, block, t, d, hf):
    s, last = t["sems_b"][hf], t["sems_b"][0] if hf else None
    W = HALF * DB
    sq = t["sq"][:].rearrange("p (i j) (h e) -> p i j h e", j=2, e=DB)
    ss, root, rn = t["ss"], t["root"], t["rn"]
    qn, kn, qc = (t["full"][:, 2 * i:2 * i + 2, :].rearrange("p i (h e) -> p i h e", e=DB) for i in range(3))
    qp = t["hi"][:, 0:4, :].rearrange("p a b -> p (a b)").rearrange("p (i h s e) -> p i h s e", i=2, s=2, e=DB)
    kp = t["lo"][:, 0:6, :].rearrange("p a b -> p (a b)").rearrange("p (i h s e) -> p i h s e", i=2, s=3, e=DB)
    ps = [[t[n][:, i * W:(i + 1) * W].rearrange("p (h e) -> p h e", e=DB) for i in range(2)] for n in ("psM0", "psM1")]
    ps.append([t[n][:].rearrange("p (h e) -> p h e", e=DB) for n in ("psO0", "psO1")])
    psX = [t[n][:].bitcast(F16).rearrange("p (h e) -> p h e", e=P) for n in ("psS0", "psS1")]

    @block.sync
    def _(sp):
        if last:
            sp.wait_ge(last["o_ready"], 2 * HALF)
        rows = d["b_krows"][hf]
        sp.dma_start(t["kb"][DB:B_ROWS, :, :], rows).then_inc(s["rows"], 16)
        sp.dma_start(t["kc"][DB:B_M, :, :], rows[0:B_M - DB]).then_inc(s["rows"], 16)
        for i in range(4):
            cols = slice(i * 2 * P, (i + 1) * 2 * P)
            sp.wait_ge(s["qa_done"], 2 * i + 2)
            sp.dma_start(t["qb"][0:DB, :, cols], t["qa"][0:DB, :, cols]).then_inc(s[f"rows{i}"], 16)
            sp.wait_ge(s["ka_done"], 2 * i + 2)
            sp.dma_start(t["kc"][0:DB, :, cols], t["ka"][0:DB, :, cols]).then_inc(s[f"rows{i}"], 16)

    @block.tensor
    def _(pe):
        m = nc.tensor
        def turn(k, j):
            part, turned = (("q_lo", "qa_turned"), ("k_lo", "ka_turned"), (None, "kb_turned"))[j]
            if part:
                pe.wait_ge(s[part], k + 1)
            if j == 1:
                pe.wait_ge(s["copied"], k + 1)
            if j == 2:
                pe.wait_ge(s["qa_done"], k + 1)
            elif k > 0:
                pe.wait_ge(s[("ka_done", "kb_done")[j]], k)
            for n in range(HALF):
                src = qp[:, k % 2, n, :, :] if j == 0 else kp[:, k % 2, n, 2 - j:4 - j, :]
                ins = m.transpose(psX[(3 * k + j) % 2][:, n, :], src.rearrange("p s e -> p (s e)"), t["identh"][:])
            ins.then_inc(s[turned], 1)

        for j in range(2 if hf else 0, 3):
            project_tile(nc, t, pe, hf, 0, j)
        for i in range(NT + 2):
            for j in range(3):
                if i >= 2:
                    turn(i - 2, j)
                if i + 1 < NT:
                    project_tile(nc, t, pe, hf, i + 1, j)

    @block.scalar
    def _(act):
        a = nc.scalar
        def take_turned(k, j):
            n = ("qa", "ka")[j]
            act.wait_ge(s[n + "_turned"], k + 1)
            a.activation(t[n][:, :, k * P:(k + 1) * P], psX[(3 * k + j) % 2][:], ACT.Copy).then_inc(s[n + "_done"], 1)

        for i in range(NT + 2):
            if i < NT:
                for j, name in enumerate(("q_sq", "k_sq")):
                    act.wait_ge(s["proj"], i * 3 + j + 1)
                    if i >= 2:
                        act.wait_ge(s["summed"], (i - 2) * 2 + j + 1)
                    a.activation(sq[:, i % 2, j], ps[j][i % 2][:], ACT.Square).then_inc(s[name], 1)
            if i >= 3:
                take_turned(i - 3, 1)
            if i < NT:
                act.wait_ge(s["proj"], i * 3 + 3)
                a.activation(t["v1"][:, i, :, 0:DB], ps[2][i % 2][:], ACT.Copy).then_inc(s["v_hi"], 1)
            if 1 <= i <= NT:
                k = i - 1
                act.wait_ge(s["k_normed"], k + 1)
                if k >= 2:
                    act.wait_ge(s["kb_turned"], k - 1)
                a.activation(kp[:, k % 2, :, 1, :], kn[:, k % 2], ACT.Copy).then_inc(s["k_hi"], 1)
                act.wait_ge(s["q_scaled"], k + 1)
                if k >= 2:
                    act.wait_ge(s["qa_turned"], k - 1)
                a.activation(qp[:, k % 2, :, 0, :], qc[:, k % 2], ACT.Copy).then_inc(s["q_hi"], 1)
            if i < NT:
                act.wait_ge(s["summed"], i * 2 + 2)
                a.activation(root[:, i % 2], ss[:, i % 2], ACT.Sqrt).then_inc(s["rooted"], 1)
            if i >= 2:
                take_turned(i - 2, 0)
        take_turned(NT - 1, 1)

    @block.gpsimd
    def _(pool):
        g = nc.gpsimd
        for i in range(NT + 1):
            if i >= 1:
                k = i - 1
                pool.wait_ge(s["k_hi"], k + 1)
                g.tensor_tensor(kp[:, k % 2, :, 0, :], kn[:, k % 2], kp[:, k % 2, :, 1, :], ALU.subtract)\
                 .then_inc(s["k_lo"], 1)
                pool.wait_ge(s["q_hi"], k + 1)
                g.tensor_tensor(qp[:, k % 2, :, 1, :], qc[:, k % 2], qp[:, k % 2, :, 0, :], ALU.subtract)\
                 .then_inc(s["q_lo"], 1)
            if i < NT:
                pool.wait_ge(s["q_normed"], i + 1)
                if i >= 2:
                    pool.wait_ge(s["q_lo"], i - 1)
                g.tensor_tensor(qc[:, i % 2], qn[:, i % 2], t["c"][:].unsqueeze(1).broadcast_to([P, HALF, DB]),
                                ALU.mult).then_inc(s["q_scaled"], 1)

    @block.vector
    def _(dve):
        v = nc.vector
        for i in range(NT + 2):
            if i < NT:
                for j, name in enumerate(("q_sq", "k_sq")):
                    dve.wait_ge(s[name], i + 1)
                    v.tensor_reduce(ss[:, i % 2, j], sq[:, i % 2, j], AX.X, ALU.add).then_inc(s["summed"], 1)
                dve.wait_ge(s["v_hi"], i + 1)
                v.tensor_tensor(t["v2"][:, i], ps[2][i % 2][:], t["v1"][:, i, :, 0:DB], ALU.subtract)\
                 .then_inc(s["v_lo"], 1)
            if 1 <= i <= NT:
                k = i - 1
                dve.wait_ge(s["k_hi"], k + 1)
                v.tensor_copy(kp[:, k % 2, :, 2, :], kp[:, k % 2, :, 1, :]).then_inc(s["copied"], 1)
            if i < NT:
                dve.wait_ge(s["rooted"], i + 1)
                v.tensor_scalar(root[:, i % 2], root[:, i % 2], 1e-12, None, ALU.max).then_inc(s["rn"], 1)
                dve.wait_ge(s["rn"], i * 2 + 1)
                v.reciprocal(rn[:, i % 2], root[:, i % 2]).then_inc(s["rn"], 1)
                dve.wait_ge(s["rn"], i * 2 + 2)
                for j, (to, name) in enumerate(((qn, "q_normed"), (kn, "k_normed"))):
                    if j == 0 and i >= 2:
                        dve.wait_ge(s["q_scaled"], i - 1)
                    if j == 1 and i >= 2:
                        dve.wait_ge(s["k_lo"], i - 1)
                    v.tensor_tensor(to[:, i % 2], ps[j][i % 2][:],
                                    rn[:, i % 2, j].unsqueeze(2).broadcast_to([P, HALF, DB]), ALU.mult)\
                     .then_inc(s[name], 1)
            if i >= 2:
                k = i - 2
                dve.wait_ge(s["kb_turned"], k + 1)
                v.tensor_copy(t["kb"][0:DB, :, k * P:(k + 1) * P], psX[(3 * k + 2) % 2][0:DB])\
                 .then_inc(s["kb_done"], 1)


def attend_b(nc, block, t, hf, last_out):
    s = t["sems_b"][hf]
    hi, lo, full = t["hi"], t["lo"], t["full"]
    nm, rest, null, nullx, nullp, nmax = (t[n] for n in ("nm", "rest", "null", "nullx", "nullp", "nmax"))
    turn, turned, rsum, warm = (t[n] for n in ("turn", "turned", "rsum", "warm"))
    psS, psM, psO = ([t[f"ps{n}{i}"] for i in range(2)] for n in "SMO")
    LO_DVE = [u for u in range(UNITS) if u not in LO_POOL]

    def unit(n, u):
        return n * UNITS + u

    def use(n, k):
        return n * USES + k

    EARLY = {6: [0], 7: [1], 8: [2]}
    LATE = {0: [3, 4], 1: [5], 5: [6]}

    def ahead(n, u):
        now = [(n + 1, k) for k in LATE.get(u, [])] + [(n + 2, k) for k in EARLY.get(u, [])]
        return [(m, k) for m, k in now if m < HALF]

    first = [(0, k) for k in range(USES)] + [(1, k) for u in sorted(EARLY) for k in EARLY[u]]
    OUT_STEPS = (0, 1, 1, 1, 1, 3, 1, 1, 0, 0)
    NULL_AT = 5

    @block.tensor
    def _(pe):
        m = nc.tensor

        def row(x, rows, n, a, b):
            return t[x][0:rows, n, a:b]

        def scores(n, par, u):
            if n == u == 0:
                pe.wait_ge(s["qa_done"], NT)
                pe.wait_ge(s["ka_done"], NT)
                pe.wait_ge(s["kb_done"], NT)
                if last_out:
                    pe.wait_ge(s["out_copied"], NT)
            if u == 0:
                pe.wait_ge(s["m_loaded"], n * 16 + 16)
            if unit(n, u) >= 2:
                pe.wait_ge(s["exp_done"], unit(n, u) * 2 - 2)
            S = psS[(par + u) % 2]
            for i, (q, kb) in enumerate(BLOCKS[4 * u:4 * u + 4]):
                out = S[:, i * P:(i + 1) * P]
                keys, queries = (kb * P, kb * P + P), (q * P, q * P + P)
                m.matmul(out, row("ka", P, n, *keys), row("qa", P, n, *queries), start=True, stop=False)
                ins = m.matmul(out, row("kb", B_ROWS, n, *keys), row("qb", B_ROWS, n, *queries),
                               start=False, stop=(q != kb))
                if q == kb:
                    ins = m.matmul(out, t["identb"][:], t["lower"][:], start=False, stop=True)
            ins.then_inc(s["s_ready"], 1)

        def max_tile(n, par, k):
            M = psM[(par + k) % 2]
            if use(n, k) == 0:
                pe.wait_ge(s["rows"], 16 * ROW_LOADS)
                pe.wait_ge(s["q_normed"], NT)
                pe.wait_ge(s["k_normed"], NT)
            if use(n, k) >= 2:
                pe.wait_ge(s["use_done"], use(n, k) - 1)
            if k == USES - 1:
                pe.wait_ge(s["null_parts"], n + 1)
                m.transpose(M[:, 0:P // 2].bitcast(F16), turn[:], t["identh"][:]).then_inc(s["use_ready"], 1)
                return
            for q, col in (MAX_TILES if n else FIRST_TILES)[k]:
                pe.wait_ge(s[f"rows{q // 2}"], 32)
                end = (q + 1) * P
                for a in range(0, end, 512):
                    z = min(end, a + 512)
                    ins = m.matmul(M[:, col + a:col + z], row("qb", B_M, n, q * P, q * P + P),
                                   row("kc", B_M, n, a, z), start=True, stop=(z < end))
                ins = m.matmul(M[:, col + q * P:col + end], t["identb"][:], t["upper"][:], start=False, stop=True)
            if k == USES - 2:
                for q in range(NT):
                    out = M[:, NULL_COL + q * NNULL:NULL_COL + (q + 1) * NNULL]
                    m.matmul(out, row("qa", P, n, q * P, q * P + P),
                             t["null_a"][:, hf * HALF + n, :], start=True, stop=False)
                    ins = m.matmul(out, row("qb", B_M, n, q * P, q * P + P),
                                   t["null_b"][:, hf * HALF + n, :], start=False, stop=True)
            ins.then_inc(s["use_ready"], 1)

        def values(n, par, u):
            if n == u == 0:
                pe.wait_ge(s["v_lo"], NT)
                if last_out:
                    pe.wait_ge(s["out_added"], 2)
            for half, first in ((0, 0), (1, 2)):
                if u == first:
                    if n > 0:
                        pe.wait_ge(s["o_done"], n * 2 + half - 1)
                    pe.wait_ge(s["use_done"], use(n, USES - 1) + 1)
                    nv = t["null_v"][:, hf * HALF + n, half * 4:half * 4 + 4, :]
                    m.matmul(psO[half][:, 0:4 * (DB + 1)], turned[0:T_M, :], nv.rearrange("p t e -> p (t e)"),
                             start=True, stop=False, skip_group_check=True)
            pe.wait_ge(s["exp_done"], unit(n, u) * 2 + 2)
            if u in LO_POOL:
                pe.wait_ge(s["lo_pool"], n * len(LO_POOL) + LO_POOL.index(u) + 1)
            else:
                pe.wait_ge(s["lo_dve"], n * len(LO_DVE) + LO_DVE.index(u) + 1)
            r = (3 * par + u) % RING
            for i, (q, kb) in enumerate(BLOCKS[4 * u:4 * u + 4]):
                out = psO[q // 4][:, q % 4 * (DB + 1):(q % 4 + 1) * (DB + 1)]
                v1, v2 = t["v1"][:, kb, n, :], t["v2"][:, kb, n, :]
                cols = slice(i * P, (i + 1) * P)
                m.matmul(out, hi[:, r, cols], v1, start=False, stop=False, skip_group_check=True)
                m.matmul(out[:, 0:DB], hi[:, r, cols], v2, start=False, stop=False, skip_group_check=True)
                ins = m.matmul(out, lo[:, r, cols], v1, start=False, stop=(q == kb), skip_group_check=True)
                if q == kb and q % 4 == 3:
                    ins.then_inc(s["o_ready"], 1)
            if u == UNITS - 1:
                pe.sem_inc(s["pv_done"], 1)
            else:
                ins.then_inc(s["pv_done"], 1)

        def head(n, par):
            for u in range(UNITS):
                scores(n, par, u)
                for h, k in ahead(n, u):
                    max_tile(h, h % 2, k)
                if u >= LAG:
                    values(n, par, u - LAG)
                elif n > 0:
                    values(n - 1, 1 - par, u - LAG + UNITS)

        step = 0
        for (h, k), n in zip(first, OUT_STEPS):
            max_tile(h, h % 2, k)
            if last_out:
                if n and step == 0:
                    pe.wait_ge(s["qa_done"], NT)
                    pe.wait_ge(s["ka_done"], NT)
                    pe.wait_ge(s["kb_done"], NT)
                    pe.wait_ge(s["v_lo"], NT)
                for i in range(step, step + n):
                    last_out.step(pe, i)
                step += n
        for n in range(HALF):
            head(n, n % 2)
        if hf == 0:
            for j in range(2):
                project_tile(nc, t, pe, 1, 0, j)
        for u in range(UNITS - LAG, UNITS):
            values(HALF - 1, 1, u)

    @block.sync
    def _(sp):
        def store_max(n):
            sp.wait_ge(s["use_done"], use(n, USES - 1) + 1)
            to = t["qb"][B_M:B_ROWS, ds(n, 1), :].rearrange("r o (q e) -> r (o q) e", e=P)
            sp.dma_start(to, turned[T_M:T_M + 3 * NT, :]).then_inc(s["m_loaded"], 16)
            sp.wait_ge(s["m_loaded"], n * 16 + 16)

        for n in range(HALF):
            store_max(n)

    @block.scalar
    def _(act):
        a = nc.scalar
        a.activation(warm[:], t["identf"][:, 0:1], ACT.Exp)

        def exp_null(n):
            act.wait_ge(s["null_sub"], n + 1)
            a.activation(nullp[:], nullx[:].rearrange("p t n -> p (t n)"), ACT.Exp).then_inc(s["null_exp"], 1)

        def head(n, par):
            for u in range(UNITS):
                act.wait_ge(s["s_ready"], unit(n, u) + 1)
                if unit(n, u) >= RING:
                    act.wait_ge(s["pv_done"], unit(n, u) - RING + 1)
                r = (3 * par + u) % RING
                for to in (hi, full):
                    a.activation(to[:, r, :], psS[(par + u) % 2][:], ACT.Exp).then_inc(s["exp_done"], 1)
                if u == 2 and n < HALF - 1:
                    exp_null(n + 1)

        if last_out:
            for i in range(NULL_AT):
                last_out.copy(act, i)
        exp_null(0)
        if last_out:
            for i in range(NULL_AT, NT):
                last_out.copy(act, i)
        for n in range(HALF):
            head(n, n % 2)

    @block.gpsimd
    def _(pool):
        p = nc.gpsimd
        p.memset(turn[:], 0.0).then_inc(s["pool_chain"], 1)

        def maximum(n):
            base = n * 6 + 1
            step = [0]

            def run(ins):
                ins.then_inc(s["pool_chain"], 1)
                step[0] += 1
                pool.wait_ge(s["pool_chain"], base + step[0])

            pool.wait_ge(s["nm_ready"], n + 1)
            pool.wait_ge(s["pool_chain"], base)
            if n > 0:
                pool.wait_ge(s["null_parts"], n)
            p.tensor_tensor(nullx[:], null[:], nm[:].unsqueeze(2).broadcast_to([P, NT, NNULL]), ALU.add)\
             .then_inc(s["null_sub"], 1)
            m1, m2, m3 = (turn[:, T_M + i * NT:T_M + (i + 1) * NT] for i in range(3))
            run(p.tensor_copy(m1, nm[:]))
            run(p.tensor_tensor(rest[:], nm[:], m1, ALU.subtract))
            run(p.tensor_copy(m2, rest[:]))
            run(p.tensor_tensor(m3, rest[:], m2, ALU.subtract))
            pool.wait_ge(s["null_exp"], n + 1)
            w = NT * NNULL
            run(p.tensor_copy(turn[:, T_P1:T_P1 + w], nullp[:]))
            run(p.tensor_copy(turn[:, T_P1B:T_P1B + w], turn[:, T_P1:T_P1 + w]))
            p.tensor_tensor(turn[:, T_P2:T_P2 + w], nullp[:], turn[:, T_P1:T_P1 + w], ALU.subtract)\
             .then_inc(s["null_parts"], 1)

        def head(n, par):
            for i, u in enumerate(LO_POOL):
                if i == len(LO_POOL) // 2 and n < HALF - 1:
                    maximum(n + 1)
                pool.wait_ge(s["exp_done"], unit(n, u) * 2 + 2)
                r = (3 * par + u) % RING
                p.tensor_tensor(lo[:, r, :], full[:, r, :], hi[:, r, :], ALU.subtract).then_inc(s["lo_pool"], 1)

        maximum(0)
        for n in range(HALF):
            head(n, n % 2)

    @block.vector
    def _(dve):
        v = nc.vector

        def max_tile(n, par, k):
            M = psM[(par + k) % 2]
            dve.wait_ge(s["use_ready"], use(n, k) + 1)
            if k == USES - 1:
                if n > 0:
                    dve.wait_ge(s["m_loaded"], n * 16)
                    dve.wait_ge(s["pv_done"], unit(n, 0) - UNITS + 3)
                v.tensor_copy(turned[:], M[:, 0:P // 2].bitcast(F16)).then_inc(s["use_done"], 1)
                return
            if k == 0 and n > 0:
                dve.wait_ge(s["null_parts"], n)
            last = k == USES - 2
            for i, (q, col) in enumerate((MAX_TILES if n else FIRST_TILES)[k]):
                ins = v.tensor_reduce(nm[:, q:q + 1], M[:, col:col + (q + 1) * P], AX.X, ALU.max, negate=True)
            if not last:
                ins.then_inc(s["use_done"], 1)
                return
            ns = M[:, NULL_COL:NULL_COL + NT * NNULL].rearrange("p (t n) -> p t n", n=NNULL)
            v.tensor_reduce(nmax[:], ns, AX.X, ALU.max, negate=True).then_inc(s["nm_chain"], 1)
            v.tensor_copy(null[:], ns).then_inc(s["use_done"], 1)
            dve.wait_ge(s["nm_chain"], n + 1)
            dve.wait_ge(s["use_done"], use(n, k) + 1)
            v.tensor_tensor(nm[:], nm[:], nmax[:], ALU.min).then_inc(s["nm_ready"], 1)

        def divide(n, half):
            o = psO[half][:, 0:4 * (DB + 1)].rearrange("p (t e) -> p t e", e=DB + 1)
            dve.wait_ge(s["o_ready"], n * 2 + half + 1)
            r = rsum[:, half * 4:half * 4 + 4]
            v.reciprocal(r, o[:, :, DB]).then_inc(s["o_inverted"], 1)
            dve.wait_ge(s["o_inverted"], n * 2 + half + 1)
            v.tensor_tensor(t["o_b"][:, half * 4:half * 4 + 4, ds(n * DB, DB)], o[:, :, 0:DB],
                            r.unsqueeze(2).broadcast_to([P, 4, DB]), ALU.mult).then_inc(s["o_done"], 1)

        def head(n, par):
            for u in range(UNITS):
                for h, k in ahead(n, u):
                    max_tile(h, h % 2, k)
                if u == 2 and n > 0:
                    divide(n - 1, 1)
                if u == 5:
                    divide(n, 0)
                if u not in LO_POOL:
                    dve.wait_ge(s["exp_done"], unit(n, u) * 2 + 2)
                    r = (3 * par + u) % RING
                    v.tensor_tensor(lo[:, r, :], full[:, r, :], hi[:, r, :], ALU.subtract).then_inc(s["lo_dve"], 1)

        for h, k in first:
            max_tile(h, h % 2, k)
        if last_out:
            for i in range(2):
                last_out.add(dve, i)
        for n in range(HALF):
            head(n, n % 2)
        divide(HALF - 1, 1)


class OutB:

    def __init__(self, nc, t, hf, b, before, psX):
        self.nc, self.t, self.s, self.hf, self.b, self.psX = nc, t, t["sems_b"][1], hf, b, psX
        self.tiles = before * NT
        self.psT = [t["psS0"], t["psS1"]]

    def step(self, pe, i):
        m, t, s = self.nc.tensor, self.t, self.s
        C = HALF * DB // P
        if i < NT:
            if i >= 2:
                pe.wait_ge(s["out_copied"], self.tiles + i - 1)
            for j in range(C):
                ins = m.transpose(self.psT[i % 2][:, j * P:(j + 1) * P], t["o_b"][:, i, j * P:(j + 1) * P],
                                  t["identf"][:])
            ins.then_inc(s["turned_out"], 1)
        if i >= 1:
            k = i - 1
            pe.wait_ge(s["out_copied"], self.tiles + k + 1)
            for j in range(C):
                ins = m.matmul(self.psX[k // 4][:, k % 4 * P:(k % 4 + 1) * P], t["oT"][:, k % 2, j * P:(j + 1) * P],
                               t["wout"][:, self.hf * C + j, :], start=(j == 0), stop=(j == C - 1))
            ins.then_inc(s["out_ready"], 1)

    def copy(self, act, i):
        act.wait_ge(self.s["turned_out"], self.tiles + i + 1)
        if i >= 2:
            act.wait_ge(self.s["out_ready"], self.tiles + i - 1)
        self.nc.scalar.activation(self.t["oT"][:, i % 2, :], self.psT[i % 2][:], ACT.Copy)\
            .then_inc(self.s["out_copied"], 1)

    def add(self, dve, i):
        dve.wait_ge(self.s["out_ready"], self.tiles + 4 * i + 4)
        x = self.t["x"][:, ds(self.b, 1), 4 * i:4 * i + 4, :].rearrange("p o t e -> p (o t e)")
        self.nc.vector.tensor_tensor(x, x, self.psX[i], ALU.add).then_inc(self.s["out_added"], 1)


def out_b(nc, block, t, out, norm):
    s = t["sems_b"][1]
    turned = ([t["psM1"][:, i * 512:(i + 1) * 512] for i in range(2)], [t["psO0"][:], t["psO1"][:]])

    @block.tensor
    def _(pe):
        pe.wait_ge(s["exp_done"], 2 * HALF * UNITS)
        pe.wait_ge(s["use_done"], HALF * USES)
        for i in range(NT + 1):
            pe.wait_ge(s["o_done"], 2 * HALF - (1 if i < NT // 2 else 0))
            out.step(pe, i)
        for j in range(2):
            norm.turn(pe, j, turned[j])

    @block.scalar
    def _(act):
        for i in range(NT):
            out.copy(act, i)
            if i in (1, 5):
                norm.root(act, i // 4)
        for j in range(2):
            norm.take(act, j, turned[j])

    @block.vector
    def _(dve):
        for i in range(2):
            norm.normalize(dve, i)
            out.add(dve, i)


def restart(nc, *sems):
    numbers = sorted(s.num for group in sems for s in group.values())
    starts = [n for n in numbers if n - 1 not in numbers]
    ends = [n + 1 for n in numbers if n + 1 not in numbers]
    with nc.Block() as block:
        @block.sync
        def _(sp):
            for start, end in zip(starts, ends):
                sp.sem_clear(range(start, end))


def attention_b(nc, t, d):
    with ExitStack() as c:
        for n, w in (("psM0", L), ("psM1", L), ("psS0", 512), ("psS1", 512), ("psO0", 512), ("psO1", 512)):
            t[n] = c.enter_context(nc.psum_tensor("b_" + n, [P, w], F32))
        norm_b(nc, t)
        restart(nc, t["sems_b"][1])
        with nc.Fori(0, B) as b:
            with nc.Block() as block:
                for hf in range(2):
                    project_b(nc, block, t, d, hf)
                    attend_b(nc, block, t, hf, OutB(nc, t, 0, b, 0, [t["psO0"][:], t["psO1"][:]]) if hf else None)
                    if hf:
                        banks = [t["psM0"][:, i * 512:(i + 1) * 512] for i in range(2)]
                        out_b(nc, block, t, OutB(nc, t, 1, b, 1, banks), NormB(nc, t, (b + 1) % B))
            restart(nc, *t["sems_b"])


def hybrid_layer(nc, d):
    def sb(c, n, s, dt): return c.enter_context(nc.sbuf_tensor(n, s, dt))
    d["parts"] = nc.dram_tensor("parts", (2 * B, 3, P, L), BF16, kind="Internal").ap()
    with ExitStack() as whole:
        t = {"identf": sb(whole, "identf", [P, P], F32), "identb": sb(whole, "identb", [P, P], BF16)}
        t["o_a"] = sb(whole, "o", [P, NT, B * HA, DA], F32)
        t["o_b"] = t["o_a"][:].rearrange("p t h e -> p t (h e)")
        with ExitStack() as c:
            t["v_a"] = sb(c, "v_a", [P, NT, B * HA, DA + 1], F32)
            with ExitStack() as first:
                t["sems_p"] = {n: first.enter_context(nc.semaphore("pa_" + n)) for n in PROJECT_SEMS}
                project_a(nc, t, d)
                restart(nc, t["sems_p"])
            attention_a(nc, t, d)
        t["x"] = sb(whole, "x", [P, B, NT, D], F32)
        t["sems_f"] = {n: whole.enter_context(nc.semaphore("ffn_" + n)) for n in FFN_SEMS}
        with ExitStack() as second:
            t.update(weights_b(nc, second))
            with ExitStack() as c:
                t.update(ffn_tiles(nc, c, "w1", True))
                ffn(nc, t, d, None, B_WEIGHTS, "f1", True)
            restart(nc, t["sems_f"])
            with ExitStack() as c:
                t.update(tiles_b(nc, c))
                load_b(nc, t, d)
                attention_b(nc, t, d)
        with ExitStack() as c:
            t.update(ffn_tiles(nc, c, "w2", False))
            ffn(nc, t, d, d["out"], (), "f2", False)



def sorted_positions():
    import numpy as np
    pos = (np.arange(L, dtype=np.float32) * np.float32((1.0 + np.sqrt(5.0)) / 2.0)) % np.float32(1.0)
    return pos, np.argsort(pos, kind="stable")


def parts_of(a, dtype, n):
    import numpy as np
    out, rest = [], np.asarray(a, np.float64)
    for _ in range(n):
        out.append(rest.astype(dtype))
        rest = rest - out[-1].astype(np.float64)
    return out


def constants():
    import numpy as np
    bf = np.dtype(mybir.dt.np(BF16))
    pos, order = sorted_positions()
    p = pos[order].astype(np.float64)
    block = np.arange(L) // P
    krows = np.zeros((A_ROWS - A_M, L), bf)
    qrows = np.zeros((A_ROWS - A_POS, L), bf)
    krows[0:3] = 1
    for r in range(NT):
        sign = np.sign(block - r).astype(np.float64)
        mid = p[block == r].mean()
        small = np.where(sign == 0, 0.0, np.log1p(1e-8 * np.exp(sign * (p - mid))))
        for s in range(3):
            krows[A_POS - A_M + 3 * r + s] = sign
            krows[A_KPOS - A_M + 3 * r + s] = parts_of(-sign * p + small, bf, 3)[s]
            qrows[3 * r + s] = np.where(block == r, parts_of(p, bf, 3)[s].astype(np.float64), 0.0)
            qrows[A_KPOS - A_POS + 3 * r + s] = block == r
    pb = p.reshape(NT, P)
    near = np.exp(-np.abs(pb[:, :, None] - pb[:, None, :])) + 1e-8
    perm = np.zeros((P, NT, L), bf)
    for i, tok in enumerate(order):
        perm[i % P, i // P, tok] = 1
    return {
        "a_krows": krows, "a_qrows": qrows,
        "near": np.ascontiguousarray(near.transpose(1, 0, 2)).astype(np.float32),
        "perm": perm, "identf": np.eye(P, dtype=np.float32), "identb": np.eye(P).astype(bf),
    }


def ffn_layout(w):
    import numpy as np
    c = np.ascontiguousarray
    return {
        "w1": c(w["W1"].T), "tw1": c(w["TW1"].transpose(2, 0, 1)),
        "w2": c(w["W2"].T.reshape(FB, P, D).transpose(1, 0, 2).reshape(P, FF)),
        "tw2": c(w["TW2"].transpose(2, 0, 1).reshape(FB, P, NE, D).transpose(1, 2, 0, 3).reshape(P, NE, FF)),
        "gw1": c(w["gate_w1"].T), "gb1": c(w["gate_b1"].reshape(P, 1)), "gw2": c(w["gate_w2"].T),
        "gb2row": c(w["gate_b2"].reshape(1, NE)), "gb2col": c(w["gate_b2"].reshape(NE, 1)),
        "b1": c(w["b1"].reshape(FB, P).T), "tb1": c(w["Tb1"].reshape(NE, FB, P).transpose(2, 1, 0)),
        "tb2": c(w["Tb2"]), "b2": c(w["b2"].reshape(1, D)),
    }


def constants_b():
    import numpy as np
    start = 2.0 ** (-2.0 ** (-(np.log2(HB) - 3)))
    slopes = np.array([start * start ** i for i in range(HB)], dtype=np.float32).astype(np.float64)
    key, block = np.arange(L), np.arange(L) // P
    krows = np.zeros((HB, B_ROWS - DB, L), np.float16)
    nrows = np.zeros((HB, B_M - DB, NNULL), np.float16)
    qrows = np.zeros((B_M - DB, L), np.float16)
    qrows[0:B_BIAS] = 1
    for h in range(HB):
        krows[h, 0:B_BIAS] = parts_of(slopes[h] * (key - P * block), np.float16, 3)
        nrows[h, 0:B_BIAS] = parts_of(slopes[h] * (np.arange(NNULL) - NNULL), np.float16, 3)
        for r in range(NT):
            at = slice(B_BIAS + 3 * r, B_BIAS + 3 * r + 3)
            krows[h, at] = parts_of(slopes[h] * P * (block - r), np.float16, 3)
            nrows[h, at] = parts_of(slopes[h] * P * (0 * np.arange(NNULL) - r), np.float16, 3)
            qrows[at] = block == r
    krows[:, B_M - DB:] = 1
    k, q = np.meshgrid(np.arange(P), np.arange(P), indexing="ij")
    diag = np.zeros((T_M, NT), np.float32)
    for first in (T_P1, T_P1B, T_P2):
        for i in range(NT):
            diag[first + NNULL * i:first + NNULL * (i + 1), i] = 1
    return {
        "b_krows": np.ascontiguousarray(krows.reshape(2, HALF, B_ROWS - DB, L).transpose(0, 2, 1, 3)),
        "b_nrows": np.ascontiguousarray(nrows.transpose(1, 0, 2)), "b_qrows": qrows, "b_diag": diag,
        "identh": np.eye(P, dtype=np.float16),
        "lower": np.where(k > q, -1e30, 0.0).astype(mybir.dt.np(BF16)),
        "upper": np.where(q > k, -1e30, 0.0).astype(mybir.dt.np(BF16)),
    }


def layout_b(w):
    import numpy as np
    c = np.ascontiguousarray
    null = w["null_kv"].reshape(HB, NNULL, 2, DB)
    null_v = np.zeros((T_M, HB, DB), np.float32)
    for first in (T_P1, T_P1B, T_P2):
        for i in range(NT):
            null_v[first + NNULL * i:first + NNULL * (i + 1)] = null[:, :, 1].transpose(1, 0, 2)
    return {
        "wq": c(w["Wq"]), "wk": c(w["Wkv"][:, :HB * DB]), "wv": c(w["Wkv"][:, HB * DB:]),
        "wout": c(w["Wout"].reshape(HB * DB // P, P, D).transpose(1, 0, 2)),
        "norm_g": c(w["norm_g"].reshape(D, 1)), "norm_b": c(w["norm_b"].reshape(D, 1)),
        "q_scale": c(w["q_scale"].reshape(1, DB)), "k_scale": c(w["k_scale"].reshape(1, DB)),
        "null_k": c(null[:, :, 0].transpose(2, 0, 1)), "null_v": null_v,
    }


def kernel(**inputs):
    import numpy as np
    import concourse.bacc as bacc
    from concourse.bass_utils import run_bass_kernel_spmd

    w = {n: np.asarray(a) for n, a in inputs.items()}
    a = {n.removeprefix("L0_attn_a_"): v for n, v in w.items() if n.startswith("L0_attn_a_")}
    b = {n.removeprefix("L0_attn_b_"): v for n, v in w.items() if n.startswith("L0_attn_b_")}
    f = {n.removeprefix("L0_ffn_"): v for n, v in w.items() if n.startswith("L0_ffn_")}
    order = sorted_positions()[1]
    arrays = {
        **constants(), **constants_b(), **layout_b(b), **ffn_layout(f),
        "x": a["x"], "x_sorted": np.ascontiguousarray(a["x"][:, order]), "w_qkv": a["w_qkv"],
        "wproj": a["w_proj"], "bproj": a["b_proj"].reshape(1, D), "ones": np.ones((1, P), np.float32),
    }
    nc = bacc.Bacc("TRN2", target_bir_lowering=False, num_devices=1)
    d = {n: nc.dram_tensor(f"in_{n}_dram", v.shape, mybir.dt.from_np(v.dtype), kind="ExternalInput").ap()
         for n, v in arrays.items()}
    d["out"] = nc.dram_tensor("out_0_dram", (B, L, D), F32, kind="ExternalOutput").ap()
    hybrid_layer(nc, d)
    r = run_bass_kernel_spmd(nc, [{f"in_{n}_dram": v for n, v in arrays.items()}], core_ids=[0])
    return r.results[0]["out_0_dram"]
```
